# Optimizing a Trainium2 kernel written in Bass

```python
import numpy as np
import jax
import jax.numpy as jnp

def _softmax(x, axis=-1):
    return jax.nn.softmax(x, axis=axis)
def _gelu(x):
    return jax.nn.gelu(x, approximate=True)
def _silu(x):
    return jax.nn.silu(x)
def _sigmoid(x):
    return jax.nn.sigmoid(x)
def _layernorm(x, axis=-1, eps=1e-5):
    m = jnp.mean(x, axis=axis, keepdims=True)
    v = jnp.var(x, axis=axis, keepdims=True)
    return (x - m) / jnp.sqrt(v + eps)
def _scatter_add(tgt, idx, src, axis=0):
    return tgt.at[idx].add(src)
def _segment_sum(src, seg, n):
    return jax.ops.segment_sum(src, seg, n)

kernel_name = 'mk_adj_resnorm_d2_adj_512_52d435'

def setup_inputs(seed: int = 0):
    np.random.seed(seed)
    _w = jnp.asarray
    def _rec_inputs():
        import jax
        import jax.numpy as jnp
        _gk = jax.random.key(seed)
        x = -1.394e-06 + 0.9999 * jax.random.normal(jax.random.fold_in(_gk, 1), (128, 128, 512), jnp.float32)
        _a = jax.random.bernoulli(jax.random.fold_in(_gk, 2), 0.125, (128, 128, 128))
        adj = _a.astype(jnp.int32)
        return x, adj
    x, adj = _rec_inputs()
    def _L0_gnn_setup():
        import jax, jax.numpy as jnp
        import numpy as np
        NEG_INF = -1000000000.0
        NEG_SLOPE = 0.2

        def gat_layer(x, mask, W, a_src, a_dst, bias, concat):
            B, N, _ = x.shape
            H, F = a_src.shape
            xl = (x @ W).reshape(B, N, H, F)
            asrc = jnp.einsum('bnhf,hf->bnh', xl, a_src)
            adst = jnp.einsum('bnhf,hf->bnh', xl, a_dst)
            e = jax.nn.leaky_relu(asrc[:, :, None, :] + adst[:, None, :, :], NEG_SLOPE)
            e = jnp.where(mask[..., None], e, NEG_INF)
            attn = jax.nn.softmax(e, axis=1)
            out = jnp.einsum('bsdh,bshf->bdhf', attn, xl)
            if concat:
                out = out.reshape(B, N, H * F)
            else:
                out = out.mean(axis=2)
            return out + bias
        key = jax.random.key(seed)
        ks = jax.random.split(key, 10)
        B, N, Din, Fh, H, Dout = (8, 1024, 512, 256, 4, 512)
        s = 0.05
        return {'adj': jax.random.randint(ks[0], (B, N, N), 0, 2, dtype=jnp.int32), 'x': jax.random.normal(ks[1], (B, N, Din), dtype=jnp.float32), 'W1': jax.random.normal(ks[2], (Din, H * Fh), dtype=jnp.float32) * s, 'att_src1': jax.random.normal(ks[3], (H, Fh), dtype=jnp.float32) * s, 'att_dst1': jax.random.normal(ks[4], (H, Fh), dtype=jnp.float32) * s, 'b1': jax.random.normal(ks[5], (H * Fh,), dtype=jnp.float32) * s, 'W2': jax.random.normal(ks[6], (H * Fh, Dout), dtype=jnp.float32) * s, 'att_src2': jax.random.normal(ks[7], (1, Dout), dtype=jnp.float32) * s, 'att_dst2': jax.random.normal(ks[8], (1, Dout), dtype=jnp.float32) * s, 'b2': jax.random.normal(ks[9], (Dout,), dtype=jnp.float32) * s}
    _L0_gnn_all = _L0_gnn_setup()
    _L0_gnn_in = {k: v for k, v in _L0_gnn_all.items() if k in ('W1', 'att_src1', 'att_dst1', 'b1', 'W2', 'att_src2', 'att_dst2', 'b2', )}
    del _L0_gnn_all

    def _L1_gnn_setup():
        import jax, jax.numpy as jnp
        import numpy as np
        ALPHA = 0.2

        def _leaky(x):
            return jnp.where(x >= 0, x, ALPHA * x)
        key = jax.random.key(seed)
        k1, k2, k3, k4 = jax.random.split(key, 4)
        B, N, F_in, F_out = (4, 2048, 512, 512)
        h = jax.random.normal(k1, (B, N, F_in), dtype=jnp.float32)
        W = jax.random.normal(k2, (F_in, F_out), dtype=jnp.float32) * 0.05
        a = jax.random.normal(k3, (2 * F_out, 1), dtype=jnp.float32) * 0.05
        adj = jax.random.randint(k4, (B, N, N), 0, 2, dtype=jnp.int32)
        return {'h': h, 'W': W, 'a': a, 'adj': adj}
    _L1_gnn_all = _L1_gnn_setup()
    _L1_gnn_in = {k: v for k, v in _L1_gnn_all.items() if k in ('W', 'a', )}
    del _L1_gnn_all

    return {
        "x": x,
        "adj": adj,
        "L0_gnn_W1": _L0_gnn_in["W1"],
        "L0_gnn_att_src1": _L0_gnn_in["att_src1"],
        "L0_gnn_att_dst1": _L0_gnn_in["att_dst1"],
        "L0_gnn_b1": _L0_gnn_in["b1"],
        "L0_gnn_W2": _L0_gnn_in["W2"],
        "L0_gnn_att_src2": _L0_gnn_in["att_src2"],
        "L0_gnn_att_dst2": _L0_gnn_in["att_dst2"],
        "L0_gnn_b2": _L0_gnn_in["b2"],
        "L1_gnn_W": _L1_gnn_in["W"],
        "L1_gnn_a": _L1_gnn_in["a"],
    }

def reference(x, adj, L0_gnn_W1, L0_gnn_att_src1, L0_gnn_att_dst1, L0_gnn_b1, L0_gnn_W2, L0_gnn_att_src2, L0_gnn_att_dst2, L0_gnn_b2, L1_gnn_W, L1_gnn_a):
    import jax
    import jax.numpy as jnp
    def _L0_gnn_ref(adj, x, W1, att_src1, att_dst1, b1, W2, att_src2, att_dst2, b2):
        import jax, jax.numpy as jnp
        import numpy as np
        NEG_INF = -1000000000.0
        NEG_SLOPE = 0.2

        def gat_layer(x, mask, W, a_src, a_dst, bias, concat):
            B, N, _ = x.shape
            H, F = a_src.shape
            xl = (x @ W).reshape(B, N, H, F)
            asrc = jnp.einsum('bnhf,hf->bnh', xl, a_src)
            adst = jnp.einsum('bnhf,hf->bnh', xl, a_dst)
            e = jax.nn.leaky_relu(asrc[:, :, None, :] + adst[:, None, :, :], NEG_SLOPE)
            e = jnp.where(mask[..., None], e, NEG_INF)
            attn = jax.nn.softmax(e, axis=1)
            out = jnp.einsum('bsdh,bshf->bdhf', attn, xl)
            if concat:
                out = out.reshape(B, N, H * F)
            else:
                out = out.mean(axis=2)
            return out + bias
        B, N, _ = adj.shape
        mask = (adj > 0) | jnp.eye(N, dtype=bool)[None]
        h = jax.nn.elu(gat_layer(x, mask, W1, att_src1, att_dst1, b1, concat=True))
        h = gat_layer(h, mask, W2, att_src2, att_dst2, b2, concat=False)
        return h

    def _L1_gnn_ref(h, W, a, adj):
        import jax, jax.numpy as jnp
        import numpy as np
        ALPHA = 0.2

        def _leaky(x):
            return jnp.where(x >= 0, x, ALPHA * x)
        F_out = W.shape[1]
        Wh = jnp.matmul(h, W)
        Wh_sg = jax.lax.stop_gradient(Wh)
        a1 = a[:F_out, 0]
        a2 = a[F_out:, 0]
        s_i = Wh_sg @ a1
        s_j = Wh_sg @ a2
        e = _leaky(s_i[:, :, None] + s_j[:, None, :])
        e = jnp.where(adj > 0, e, jnp.float32(-9000000000000000.0))
        attention = jax.nn.softmax(e, axis=1)
        h_prime = jnp.einsum('bij,bjf->bif', attention, Wh)
        return _leaky(h_prime)

    x = _layernorm(x + _L0_gnn_ref(adj, x, L0_gnn_W1, L0_gnn_att_src1, L0_gnn_att_dst1, L0_gnn_b1, L0_gnn_W2, L0_gnn_att_src2, L0_gnn_att_dst2, L0_gnn_b2), axis=-1)
    x = _layernorm(x + _L1_gnn_ref(x, L1_gnn_W, L1_gnn_a, adj), axis=-1)
    return x


_drawn_inputs = setup_inputs


def setup_inputs(seed=0):
    import zlib

    import numpy as np

    out = dict(_drawn_inputs(seed))
    spreads = {}
    factors = {'L0_gnn_att_dst2': 3.323}
    for name, (base, spread) in spreads.items():
        noise = np.random.default_rng([zlib.crc32(name.encode()), seed]).standard_normal(out[name].shape)
        drawn = base * np.exp(spread * noise) if base else spread * noise
        out[name] = jnp.asarray(drawn.astype(out[name].dtype))
    for name, factor in factors.items():
        out[name] = (out[name] * factor).astype(out[name].dtype)
    return out
```

```python
from contextlib import ExitStack

import concourse.bass as bass
from concourse import mybir

F32 = mybir.dt.float32
F32R = mybir.dt.float32r
BF16 = mybir.dt.bfloat16
I32 = mybir.dt.int32
ALU = mybir.AluOpType
ACT = mybir.ActivationFunctionType
AX = mybir.AxisListType

P = 128
MASKED = -9e15
SLOPE = 0.2
EPS = 1e-5


def resnorm_gat_kernel(nc, x, x_t, adj_t, w1, a_src1, a_dst1, b1, w2, a_src2, a_dst2, b2, w3, a3, out):
    B, N, D = x.shape
    H, F = a_src1.shape
    HF = H * F
    assert N == P and D % P == 0 and F == 256 and D == 512
    KT1, KT2, KT3 = D // P, HF // P, D // P
    C1 = HF + 2 * H
    C1P = C1 // 3
    C2 = D + 4
    C2P = C2 // 2
    S1 = HF - 2 * C1P
    S2 = D - C2P

    LOOP_FROM, LOOP_TO, STEPS = 6, B - 4, B + 3

    with ExitStack() as ctx:
        def sb(name, shape, dt=F32):
            return ctx.enter_context(nc.sbuf_tensor(name, shape, dt))

        def sem(name):
            return ctx.enter_context(nc.semaphore(name))

        ident = sb("ident", [P, P])
        ident_b = sb("ident_b", [P, P], BF16)
        not_eye = sb("not_eye", [P, P], BF16)
        w1_hi, w1_lo = sb("w1_hi", [P, KT1, C1], F32R), sb("w1_lo", [P, KT1, C1], F32R)
        w2_hi, w2_lo = sb("w2_hi", [P, KT2, C2], F32R), sb("w2_lo", [P, KT2, C2], F32R)
        w3_hi, w3_lo = sb("w3_hi", [P, KT3, C2], F32R), sb("w3_lo", [P, KT3, C2], F32R)
        b1_rows = sb("b1_rows", [P, C1])
        b2_rows = sb("b2_rows", [P, D])
        w_raw = sb("w_raw", [P, 2, C1])

        xt = sb("xt", [P, 2, D])
        xt_hi, xt_lo = sb("xt_hi", [P, 2, D], F32R), sb("xt_lo", [P, 2, D], F32R)
        x_in, x_b2 = sb("x_in", [P, 2, D]), sb("x_b2", [P, 2, D])
        adj = sb("adj", [P, 2, N], I32)
        mask0, mask1 = sb("mask0", [P, 2, N], BF16), sb("mask1", [P, 2, N], BF16)
        mask_t = sb("mask_t", [P, N], BF16)
        att1, att2, att3 = sb("att1", [P, 2 * H]), sb("att2", [P, 2]), sb("att3", [P, 2])
        xl = sb("xl", [P, C1])
        xl_hi, xl_lo = sb("xl_hi", [P, HF], F32R), sb("xl_lo", [P, HF], F32R)
        z1, e1, p1 = sb("z1", [P, H, N]), sb("e1", [P, H, N]), sb("p1", [P, H, N])
        p1_hi, p1_lo = sb("p1_hi", [P, H, N], F32R), sb("p1_lo", [P, H, N], F32R)
        top1, ntop1, nmax1 = sb("top1", [P, H]), sb("ntop1", [P, H]), sb("nmax1", [P, H])
        den1, rden1 = sb("den1", [P, H]), sb("rden1", [P, H])
        ex, exm, h = sb("ex", [P, HF]), sb("exm", [P, HF]), sb("h", [P, HF])
        ht_hi, ht_lo = sb("ht_hi", [P, HF], F32R), sb("ht_lo", [P, HF], F32R)
        x2_hi, x2_lo = sb("x2_hi", [P, C2], F32R), sb("x2_lo", [P, C2], F32R)
        z2, e2, p2 = sb("z2", [P, N]), sb("e2", [P, N]), sb("p2", [P, N])
        p2_hi, p2_lo = sb("p2_hi", [P, N], F32R), sb("p2_lo", [P, N], F32R)
        top2, ntop2, nmax2 = sb("top2", [P, 1]), sb("ntop2", [P, 1]), sb("nmax2", [P, 1])
        den2, rden2 = sb("den2", [P, 1]), sb("rden2", [P, 1])
        y2, x1 = sb("y2", [P, D]), sb("x1", [P, 2, D])
        x1_hi, x1_lo = sb("x1_hi", [P, D], F32R), sb("x1_lo", [P, D], F32R)
        wh_hi, wh_lo = sb("wh_hi", [P, C2], F32R), sb("wh_lo", [P, C2], F32R)
        z3, e3, p3 = sb("z3", [P, N]), sb("e3", [P, N]), sb("p3", [P, N])
        p3_hi, p3_lo = sb("p3_hi", [P, N], F32R), sb("p3_lo", [P, N], F32R)
        top3, ntop3, nmax3 = sb("top3", [P, 1]), sb("ntop3", [P, 1]), sb("nmax3", [P, 1])
        den3, rden3 = sb("den3", [P, 1]), sb("rden3", [P, 1])
        relu3, x1_relu3, y3 = sb("relu3", [P, D]), sb("x1_relu3", [P, D]), sb("y3", [P, D])
        res = sb("res", [P, 2, D])
        ln2, ln3 = sb("ln2", [P, 16]), sb("ln3", [P, 16])

        wide = ctx.enter_context(nc.psum_tensor("wide", [P, 3, 512], F32))
        pair = ctx.enter_context(nc.psum_tensor("pair", [P, 2, 512], F32))
        heads = ctx.enter_context(nc.psum_tensor("heads", [P, 2, 512], F32))
        score = ctx.enter_context(nc.psum_tensor("score", [P, 512], F32))

        vectors_in, bias_in = sem("vectors_in"), sem("bias_in")
        raw_in, xt_in, x_in_s, adj_in, res_out = (
            [sem(f"{n}_{c}") for c in range(2)] for n in ("raw_in", "xt_in", "x_in_s", "adj_in", "res_out"))
        ident_zero, ident_made, consts_made = sem("ident_zero"), sem("ident_made"), sem("consts_made")
        raw_pads, product_used, raw_att, w_hi_made, w_lo_made = sem("raw_pads"), sem("product_used"), sem("raw_att"), sem("w_hi_made"), sem("w_lo_made")
        (xt_hi_s, xt_lo_s, x_b2_s, mask_t_s, mask0_s, mask1_s) = map(
            sem, ("xt_hi_s", "xt_lo_s", "x_b2_s", "mask_t_s", "mask0_s", "mask1_s"))
        (xw1_s, bcast1_s, pt1_s, av1_s, ht_s) = map(sem, ("xw1_s", "bcast1_s", "pt1_s", "av1_s", "ht_s"))
        (hw2_s, bcast2_s, pt2_s, av2_s, x1t_s) = map(sem, ("hw2_s", "bcast2_s", "pt2_s", "av2_s", "x1t_s"))
        (xw3_s, bcast3_s, av3_s) = map(sem, ("xw3_s", "bcast3_s", "av3_s"))
        (att1_s, xl_s, xl_hi_s, xl_lo_s) = map(sem, ("att1_s", "xl_s", "xl_hi_s", "xl_lo_s"))
        (top1_s, ntop1_s, nmax1_s, z1_s, e1_s, p1_s, rden1_s, p1_hi_s, p1_lo_s) = map(
            sem, ("top1_s", "ntop1_s", "nmax1_s", "z1_s", "e1_s", "p1_s", "rden1_s", "p1_hi_s", "p1_lo_s"))
        (ex_s, exm_s, h_s, ht_hi_s, ht_lo_s) = map(sem, ("ex_s", "exm_s", "h_s", "ht_hi_s", "ht_lo_s"))
        (att2_s, x2_hi_s, x2_lo_s, top2_s, ntop2_s, nmax2_s, z2_s, e2_s, p2_s, rden2_s, p2_hi_s, p2_lo_s) = map(
            sem, ("att2_s", "x2_hi_s", "x2_lo_s", "top2_s", "ntop2_s", "nmax2_s", "z2_s", "e2_s", "p2_s",
                  "rden2_s", "p2_hi_s", "p2_lo_s"))
        (y2_s, bn2_s, mv2_s, ve2_s, lnv2_s, guess2_s, step2_s, factor2_s, rstd2_s, x1_s, x1_hi_s, x1_lo_s) = map(
            sem, ("y2_s", "bn2_s", "mv2_s", "ve2_s", "lnv2_s", "guess2_s", "step2_s", "factor2_s", "rstd2_s",
                  "x1_s", "x1_hi_s", "x1_lo_s"))
        (att3_s, wh_hi_s, wh_lo_s, top3_s, ntop3_s, nmax3_s, z3_s, e3_s, p3_s, rden3_s, p3_hi_s, p3_lo_s) = map(
            sem, ("att3_s", "wh_hi_s", "wh_lo_s", "top3_s", "ntop3_s", "nmax3_s", "z3_s", "e3_s", "p3_s",
                  "rden3_s", "p3_hi_s", "p3_lo_s"))
        (relu3_s, x1_relu3_s, y3_s, bn3_s, mv3_s, ve3_s, lnv3_s, guess3_s, step3_s, factor3_s, rstd3_s, res_s) = map(
            sem, ("relu3_s", "x1_relu3_s", "y3_s", "bn3_s", "mv3_s", "ve3_s", "lnv3_s", "guess3_s", "step3_s",
                  "factor3_s", "rstd3_s", "res_s"))

        def live(g):
            return not isinstance(g, int) or 0 <= g < B

        def wait(eng, s, g, per=1, short=0):
            if not isinstance(g, int) or g >= 0:
                eng.wait_ge(s, g * per + (per - short))

        def wait_dma(eng, s, g, c):
            if not isinstance(g, int) or g >= 0:
                eng.wait_ge(s[c], 8 * g + (16 - 8 * c))

        def run(eng, step):
            for i in range(LOOP_FROM):
                step(i, i % 2)
            with eng.Fori(LOOP_FROM, LOOP_TO, 2) as i:
                step(i, 0)
                step(i + 1, 1)
            for i in range(LOOP_TO, STEPS):
                step(i, i % 2)

        def weight_tiles():
            for kt in range(KT1):
                yield "w1", kt, C1, w1_hi[:, kt, :], w1_lo[:, kt, :], w1
            for kt in range(KT2):
                yield "w2", kt, C2, w2_hi[:, kt, :], w2_lo[:, kt, :], w2
            for kt in range(KT3):
                yield "w3", kt, C2, w3_hi[:, kt, :], w3_lo[:, kt, :], w3
        TILES = KT1 + KT2 + KT3
        a_src1_rows, a_dst1_rows = h, exm
        a2_rows, a3_rows = res, x1

        block = ctx.enter_context(nc.Block())

        @block.sync
        def _(sp):
            def rows(v, n):
                return v.unsqueeze(0).broadcast_to([P, n])
            sp.dma_start(a_src1_rows[:, :], rows(a_src1.rearrange("h f -> (h f)"), HF)).then_inc(vectors_in, 16)
            sp.dma_start(a_dst1_rows[:, :], rows(a_dst1.rearrange("h f -> (h f)"), HF)).then_inc(vectors_in, 16)
            sp.dma_start(a2_rows[:, 0, :], rows(a_src2.rearrange("h f -> (h f)"), D)).then_inc(vectors_in, 16)
            sp.dma_start(a2_rows[:, 1, :], rows(a_dst2.rearrange("h f -> (h f)"), D)).then_inc(vectors_in, 16)
            sp.dma_start(a3_rows[:, :, :].rearrange("p a b -> p (a b)"), rows(a3.rearrange("f o -> (f o)"), 2 * D)).then_inc(vectors_in, 16)
            for t, (_n, kt, cols, _hi, _lo, src) in enumerate(weight_tiles()):
                if t >= 2:
                    sp.wait_ge(w_hi_made, t - 1)
                    sp.wait_ge(w_lo_made, t - 1)
                n = src.shape[1]
                sp.dma_start(w_raw[:, t % 2, 0:n], src[kt * P:(kt + 1) * P, :]).then_inc(raw_in[t % 2], 16)
                if t == 1:
                    sp.dma_start(b1_rows[:, 0:HF], rows(b1, HF)).then_inc(bias_in, 16)
                    sp.dma_start(b2_rows[:, :], rows(b2, D)).then_inc(bias_in, 16)

            def load_xt(g, c):
                if live(g):
                    wait(sp, xt_hi_s, g - 2)
                    wait(sp, xt_lo_s, g - 2)
                    sp.dma_start(xt[:, c, :], x_t[g]).then_inc(xt_in[c], 16)

            def load_x(g, c):
                if live(g):
                    wait(sp, x_b2_s, g - 2)
                    sp.dma_start(x_in[:, c, :], x[g]).then_inc(x_in_s[c], 16)

            def load_adj(g, c):
                if live(g):
                    wait(sp, mask_t_s, g - 2)
                    wait(sp, mask1_s, g - 2)
                    sp.dma_start(adj[:, c, :], adj_t[g]).then_inc(adj_in[c], 16)

            def step(i, c):
                if isinstance(i, int) and i == 0:
                    for g in range(2):
                        load_xt(g, g)
                    load_adj(0, 0)
                load_x(i, c)
                load_xt(i + 2, c)
                load_adj(i + 1, 1 - c)
                g = i - 3
                if live(g):
                    wait(sp, res_s, g)
                    sp.dma_start(out[g], res[:, 1 - c, :]).then_inc(res_out[1 - c], 16)

            run(sp, step)
            for c in range(2):
                sp.wait_ge(res_out[c], 16 * (B // 2))

        @block.tensor
        def _(pe):
            pe.wait_ge(consts_made, 1)

            def split_matmul(dst, k, kts, lhs, rhs, last=None):
                n = 0
                for a, b in ((0, 0), (0, 1), (1, 0)):
                    for ch, d in enumerate(dst):
                        mm = pe.matmul(d, lhs[a], rhs[b](ch), start=(k == 0 and n == 0),
                                       stop=(k == kts - 1 and n == 2), skip_group_check=True)
                    n += 1
                return mm

            def xw1(g, c, kts):
                if not live(g):
                    return
                if kts[0] == 0:
                    if isinstance(g, int) and g == 0:
                        pe.wait_ge(w_hi_made, KT1)
                        pe.wait_ge(w_lo_made, KT1)
                    wait(pe, xt_hi_s, g)
                    wait(pe, xt_lo_s, g)
                    wait(pe, wh_hi_s, g - 3)
                    wait(pe, wh_lo_s, g - 3)
                for k in kts:
                    mm = split_matmul(
                        [wide[:, ch, 0:C1P] for ch in range(3)], k, KT1,
                        (xt_hi[:, c, k * P:(k + 1) * P], xt_lo[:, c, k * P:(k + 1) * P]),
                        (lambda ch: w1_hi[:, k, ch * C1P:(ch + 1) * C1P],
                         lambda ch: w1_lo[:, k, ch * C1P:(ch + 1) * C1P]))
                if kts[-1] == KT1 - 1:
                    mm.then_inc(xw1_s, 1)

            def hw2(g, kts):
                if not live(g):
                    return
                if kts[0] == 0:
                    if isinstance(g, int) and g == 0:
                        pe.wait_ge(w_hi_made, KT1 + KT2)
                        pe.wait_ge(w_lo_made, KT1 + KT2)
                    wait(pe, y3_s, g - 2)
                    wait(pe, x1_lo_s, g - 1)
                for k in kts:
                    if k in (0, KT2 // 2):
                        half = 1 if k == 0 else 0
                        wait(pe, ht_hi_s, g, 2, half)
                        wait(pe, ht_lo_s, g, 2, half)
                    mm = split_matmul(
                        [pair[:, ch, 0:C2P] for ch in range(2)], k, KT2,
                        (ht_hi[:, k * P:(k + 1) * P], ht_lo[:, k * P:(k + 1) * P]),
                        (lambda ch: w2_hi[:, k, ch * C2P:(ch + 1) * C2P],
                         lambda ch: w2_lo[:, k, ch * C2P:(ch + 1) * C2P]))
                if kts[-1] == KT2 - 1:
                    mm.then_inc(hw2_s, 1)

            def xw3(g, kts):
                if not live(g):
                    return
                if kts[0] == 0:
                    if isinstance(g, int) and g == 0:
                        pe.wait_ge(w_hi_made, TILES)
                        pe.wait_ge(w_lo_made, TILES)
                    wait(pe, x1_hi_s, g)
                    wait(pe, x1_lo_s, g)
                    if not isinstance(g, int) or g + 2 < B:
                        wait(pe, xl_s, g + 2)
                for k in kts:
                    mm = split_matmul(
                        [wide[:, ch, 0:C2P] for ch in range(2)], k, KT3,
                        (x1_hi[:, k * P:(k + 1) * P], x1_lo[:, k * P:(k + 1) * P]),
                        (lambda ch: w3_hi[:, k, ch * C2P:(ch + 1) * C2P],
                         lambda ch: w3_lo[:, k, ch * C2P:(ch + 1) * C2P]))
                if kts[-1] == KT3 - 1:
                    mm.then_inc(xw3_s, 1)

            def spread(dst, col, mask, n, done):
                for k in range(n):
                    pe.matmul(dst[:, k * N:(k + 1) * N], col[:, k:k + 1].broadcast_to([P, P]), ident[:, :],
                              is_transpose=True, start=(k == 0), stop=False, skip_group_check=True)
                pe.matmul(dst[:, 0:n * N].rearrange("p (k s) -> p k s", k=n), ident_b[:, :],
                          mask.unsqueeze(1).broadcast_to([P, n, N]), start=False, stop=True,
                          skip_group_check=True).then_inc(done, 1)

            def bcast1(g, c):
                if live(g):
                    wait(pe, att1_s, g)
                    wait(pe, mask0_s, g)
                    wait(pe, p2_lo_s, g - 2)
                    spread(score, att1, mask0[:, c, :], H, bcast1_s)

            def bcast2(g, c):
                if live(g):
                    wait(pe, att2_s, g)
                    if not isinstance(g, int) or g + 1 < B:
                        wait(pe, p1_lo_s, g + 1)
                    spread(score, att2, mask0[:, c, :], 1, bcast2_s)

            def bcast3(g, c):
                if live(g):
                    wait(pe, att3_s, g)
                    wait(pe, mask1_s, g)
                    spread(pair[:, 1, :], att3, mask1[:, c, :], 1, bcast3_s)

            def pt1(g):
                if live(g):
                    wait(pe, p1_s, g, H)
                    for k in range(H):
                        mm = pe.transpose(score[:, k * N:(k + 1) * N], p1[:, k, :], ident[:, :])
                    mm.then_inc(pt1_s, 1)

            def pt2(g):
                if live(g):
                    wait(pe, p2_s, g)
                    pe.transpose(score[:, 0:N], p2[:, :], ident[:, :]).then_inc(pt2_s, 1)

            def av1(g):
                if live(g):
                    wait(pe, p1_hi_s, g)
                    wait(pe, p1_lo_s, g)
                    wait(pe, xl_hi_s, g)
                    wait(pe, xl_lo_s, g)
                    for k in range(H):
                        dst = heads[:, k // 2, (k % 2) * F:(k % 2 + 1) * F]
                        cols = slice(k * F, (k + 1) * F)
                        for n, (a, b) in enumerate(((p1_hi, xl_hi), (p1_hi, xl_lo), (p1_lo, xl_hi))):
                            mm = pe.matmul(dst, a[:, k, :], b[:, cols], start=(n == 0), stop=(n == 2),
                                           skip_group_check=True)
                        if k % 2 == 1:
                            mm.then_inc(av1_s, 1)

            def ht(g):
                if live(g):
                    for half in range(2):
                        wait(pe, h_s, g, 2, 0)
                        for k in range(4):
                            f = half * 4 + k
                            mm = pe.transpose(heads[:, half, k * P:(k + 1) * P], h[:, f * P:(f + 1) * P],
                                              ident[:, :])
                        mm.then_inc(ht_s, 1)

            def av_wide(dst, p_hi, p_lo, v_hi, v_lo, done):
                for n, (a, b) in enumerate(((p_hi, v_hi), (p_hi, v_lo), (p_lo, v_hi))):
                    mm = pe.matmul(dst, a[:, :], b[:, 0:D], start=(n == 0), stop=(n == 2))
                mm.then_inc(done, 1)

            def av2(g):
                if live(g):
                    wait(pe, p2_hi_s, g)
                    wait(pe, p2_lo_s, g)
                    wait(pe, x2_hi_s, g)
                    wait(pe, x2_lo_s, g)
                    av_wide(pair[:, 0, :], p2_hi, p2_lo, x2_hi, x2_lo, av2_s)

            def x1t(g):
                if live(g):
                    wait(pe, x1_s, g)
                    wait(pe, z3_s, g - 1)
                    wait(pe, top3_s, g - 1)
                    for k in range(KT3):
                        mm = pe.transpose(pair[:, 1, k * P:(k + 1) * P], x1[:, c2(g), k * P:(k + 1) * P],
                                          ident[:, :])
                    mm.then_inc(x1t_s, 1)

            def av3(g):
                if live(g):
                    wait(pe, p3_hi_s, g)
                    wait(pe, p3_lo_s, g)
                    wait(pe, wh_hi_s, g)
                    wait(pe, wh_lo_s, g)
                    if not isinstance(g, int) or g + 1 < B:
                        wait(pe, y2_s, g + 1)
                    av_wide(pair[:, 0, :], p3_hi, p3_lo, wh_hi, wh_lo, av3_s)

            parity = [0]

            def c2(g):
                return parity[0]

            def step(i, c):
                parity[0] = c
                xw1(i, c, [0])
                bcast3(i - 3, 1 - c)
                xw1(i, c, [1, 2])
                x1t(i - 2)
                ht(i - 1)
                av3(i - 3)
                xw1(i, c, [3])
                hw2(i - 1, [0, 1])
                bcast1(i, c)
                hw2(i - 1, [2, 3, 4, 5, 6, 7])
                pt1(i)
                xw3(i - 2, [0, 1])
                bcast2(i - 1, 1 - c)
                av1(i)
                xw3(i - 2, [2])
                pt2(i - 1)
                xw3(i - 2, [3])
                av2(i - 1)

            run(pe, step)

        @block.scalar
        def _(act):
            for t, (_n, kt, cols, hi, _lo, _src) in enumerate(weight_tiles()):
                act.wait_ge(raw_att, t + 1)
                act.activation(hi, w_raw[:, t % 2, 0:cols], ACT.Copy).then_inc(w_hi_made, 1)

            def wh_halves(g):
                if live(g):
                    wait(act, att3_s, g)
                    wait(act, av3_s, g - 1)
                    act.activation(wh_hi[:, :].rearrange("p (a b) -> p a b", a=2), wide[:, 0:2, 0:C2P],
                                   ACT.Copy).then_inc(wh_hi_s, 1)

            def exp3(g):
                if live(g):
                    wait(act, e3_s, g)
                    wait(act, nmax3_s, g)
                    wait(act, p3_lo_s, g - 1)
                    wait(act, rden3_s, g - 1)
                    act.activation(p3[:, :], e3[:, :], ACT.Exp, bias=nmax3[:, 0:1],
                                   accum_out=den3[:, 0:1]).then_inc(p3_s, 1)
                    wait(act, rden3_s, g)
                    wait(act, av3_s, g - 1)
                    act.activation(p3_hi[:, :], p3[:, :], ACT.Copy, scale=rden3[:, 0:1]).then_inc(p3_hi_s, 1)

            def x1_halves(g):
                if live(g):
                    wait(act, x1t_s, g)
                    wait(act, xw3_s, g - 1)
                    act.activation(x1_hi[:, :], pair[:, 1, :], ACT.Copy).then_inc(x1_hi_s, 1)

            def ht_halves(g):
                if live(g):
                    for half in range(2):
                        wait(act, ht_s, g, 2, 1 - half)
                        wait(act, hw2_s, g - 1)
                        act.activation(ht_hi[:, half * 512:(half + 1) * 512], heads[:, half, :],
                                       ACT.Copy).then_inc(ht_hi_s, 1)

            def xt_halves(g, c):
                if live(g):
                    wait_dma(act, xt_in, g, c)
                    wait(act, xw1_s, g - 2)
                    act.activation(xt_hi[:, c, :], xt[:, c, :], ACT.Copy).then_inc(xt_hi_s, 1)

            def root_guess(g, ln, ve_s, lnv_s, guess_s):
                if live(g):
                    wait(act, ve_s, g)
                    act.activation(ln[:, 9:10], ln[:, 8:9], ACT.Ln).then_inc(lnv_s, 1)
                    wait(act, lnv_s, g)
                    act.activation(ln[:, 10:11], ln[:, 9:10], ACT.Exp, scale=-0.5).then_inc(guess_s, 1)

            def relu_part3(g):
                if live(g):
                    wait(act, av3_s, g)
                    wait(act, x1_relu3_s, g - 1)
                    act.activation(relu3[:, :], pair[:, 0, :], ACT.Relu, scale=1.0 - SLOPE).then_inc(relu3_s, 1)

            def xl_halves(g):
                if live(g):
                    wait(act, xl_s, g)
                    wait(act, av1_s, g - 1, 2)
                    act.activation(xl_hi[:, :], xl[:, 0:HF], ACT.Copy).then_inc(xl_hi_s, 1)

            def exp1(g):
                if live(g):
                    wait(act, e1_s, g)
                    wait(act, nmax1_s, g)
                    wait(act, pt1_s, g - 1)
                    wait(act, rden1_s, g - 1)
                    for k in range(H):
                        act.activation(p1[:, k, :], e1[:, k, :], ACT.Exp, bias=nmax1[:, k:k + 1],
                                       accum_out=den1[:, k:k + 1]).then_inc(p1_s, 1)

            def p1_halves(g):
                if live(g):
                    wait(act, pt1_s, g)
                    wait(act, av1_s, g - 1, 2)
                    act.activation(p1_hi[:, :, :].rearrange("p a b -> p (a b)"), score[:, :],
                                   ACT.Copy).then_inc(p1_hi_s, 1)

            def x2_halves(g):
                if live(g):
                    wait(act, att2_s, g)
                    wait(act, av2_s, g - 1)
                    act.activation(x2_hi[:, :].rearrange("p (a b) -> p a b", a=2), pair[:, :, 0:C2P],
                                   ACT.Copy).then_inc(x2_hi_s, 1)

            def exp2(g):
                if live(g):
                    wait(act, e2_s, g)
                    wait(act, nmax2_s, g)
                    wait(act, pt2_s, g - 1)
                    wait(act, rden2_s, g - 1)
                    act.activation(p2[:, :], e2[:, :], ACT.Exp, bias=nmax2[:, 0:1],
                                   accum_out=den2[:, 0:1]).then_inc(p2_s, 1)

            def p2_halves(g):
                if live(g):
                    wait(act, pt2_s, g)
                    wait(act, av2_s, g - 1)
                    act.activation(p2_hi[:, :], score[:, 0:N], ACT.Copy).then_inc(p2_hi_s, 1)

            def elu_exp(g, banks):
                if live(g):
                    wait(act, rden1_s, g)
                    wait(act, exm_s, g - 1, 2)
                    for b in banks:
                        wait(act, av1_s, g, 2, 1 - b)
                        for k in (2 * b, 2 * b + 1):
                            last = act.activation(ex[:, k * F:(k + 1) * F],
                                                  heads[:, b, (k % 2) * F:(k % 2 + 1) * F],
                                                  ACT.Exp, scale=rden1[:, k:k + 1])
                        last.then_inc(ex_s, 1)

            def step(i, c):
                if isinstance(i, int) and i == 0:
                    xt_halves(0, 0)
                wh_halves(i - 3)
                root_guess(i - 2, ln2, ve2_s, lnv2_s, guess2_s)
                exp3(i - 3)
                x1_halves(i - 2)
                ht_halves(i - 1)
                relu_part3(i - 3)
                xl_halves(i)
                root_guess(i - 3, ln3, ve3_s, lnv3_s, guess3_s)
                exp1(i)
                xt_halves(i + 1, 1 - c)
                x2_halves(i - 1)
                p1_halves(i)
                exp2(i - 1)
                elu_exp(i, [0])
                p2_halves(i - 1)
                elu_exp(i, [1])

            run(act, step)

        @block.vector
        def _(dve):
            dve.wait_ge(vectors_in, 5 * 16)
            dve.memset(b1_rows[:, HF:C1], 0.0).then_inc(raw_pads, 1)
            product = 0
            for t, (name, kt, cols, _hi, _lo, _src) in enumerate(weight_tiles()):
                raw = w_raw[:, t % 2, :]
                dve.wait_ge(raw_in[t % 2], 16 * (t // 2 + 1))
                if name == "w1":
                    vecs = [(rows[:, k * F:(k + 1) * F], k * F, F)
                            for rows in (a_src1_rows, a_dst1_rows) for k in range(H)]
                    base = HF
                else:
                    rows = a2_rows if name == "w2" else a3_rows
                    vecs = [(rows[:, j, :], 0, D) for j in range(2)]
                    base = D
                if name != "w1":
                    if t >= 2:
                        dve.wait_ge(w_hi_made, t - 1)
                        dve.wait_ge(w_lo_made, t - 1)
                    dve.memset(raw[:, base + 2:base + 4], 0.0)
                for j, (vec, at, n) in enumerate(vecs):
                    if j >= HF // n:
                        dve.wait_ge(product_used, product)
                    product += 1
                    scratch = ex[:, j * n % HF:j * n % HF + n]
                    dve.tensor_tensor_reduce(scratch, raw[:, at:at + n], vec, 1.0, 0.0, ALU.mult, ALU.add,
                                             raw[:, base + j:base + j + 1]).then_inc(product_used, 1)
                dve.wait_ge(product_used, product)
                dve.sem_inc(raw_att, 1)
                dve.wait_ge(raw_att, t + 1)
            dve.wait_ge(bias_in, 2 * 16)

            def top_of(dst, src, bc_s, top_s, g, n):
                wait(dve, bc_s, g)
                dve.tensor_reduce(dst[:, 0:n], src, AX.X, ALU.max).then_inc(top_s, 1)

            def negative_max(g, top, dst_col, ntop, nmax, top_s, ntop_s, nmax_s, p_s, per):
                wait(dve, top_s, g)
                dve.scalar_tensor_tensor(out=ntop[:, :], in0=top[:, :], scalar=-1.0, in1=dst_col,
                                         op0=ALU.mult, op1=ALU.subtract).then_inc(ntop_s, 1)
                wait(dve, ntop_s, g)
                wait(dve, p_s, g - 1, per)
                dve.scalar_tensor_tensor(out=nmax[:, :], in0=ntop[:, :], scalar=SLOPE, in1=ntop[:, :],
                                         op0=ALU.mult, op1=ALU.min).then_inc(nmax_s, 1)

            def mask_of(dst, g, c, done):
                wait_dma(dve, adj_in, g, c)
                dve.tensor_scalar(dst, adj[:, c, :], 0.0, MASKED, ALU.is_le, ALU.mult).then_inc(done, 1)

            def make_mask1(g, c):
                if live(g):
                    wait(dve, bcast3_s, g - 2)
                    mask_of(mask1[:, c, :], g, c, mask1_s)

            def make_mask_t(g, c):
                if live(g):
                    wait(dve, mask0_s, g - 1)
                    mask_of(mask_t[:, :], g, c, mask_t_s)

            def att_wh(g):
                if live(g):
                    wait(dve, xw3_s, g)
                    dve.tensor_copy(att3[:, :], wide[:, 1, S2:S2 + 2]).then_inc(att3_s, 1)

            def wh_rest(g):
                if live(g):
                    wait(dve, wh_hi_s, g)
                    wait(dve, av3_s, g - 1)
                    dve.tensor_tensor(wh_lo[:, :].rearrange("p (a b) -> p a b", a=2), wide[:, 0:2, 0:C2P],
                                      wh_hi[:, :].rearrange("p (a b) -> p a b", a=2),
                                      ALU.subtract).then_inc(wh_lo_s, 1)

            def elu(g):
                if live(g):
                    for b in range(2):
                        wait(dve, ex_s, g, 2, 1 - b)
                        wait(dve, h_s, g - 1, 2)
                        dve.tensor_scalar(exm[:, b * 512:(b + 1) * 512], ex[:, b * 512:(b + 1) * 512], 1.0, -1.0,
                                          ALU.min, ALU.add).then_inc(exm_s, 1)
                        wait(dve, exm_s, g, 2, 1 - b)
                        wait(dve, ht_s, g - 1, 2)
                        for k in (2 * b, 2 * b + 1):
                            last = dve.scalar_tensor_tensor(
                                out=h[:, k * F:(k + 1) * F], in0=heads[:, b, (k % 2) * F:(k % 2 + 1) * F],
                                scalar=rden1[:, k:k + 1], in1=exm[:, k * F:(k + 1) * F],
                                op0=ALU.mult, op1=ALU.max)
                        last.then_inc(h_s, 1)

            def scores3(g):
                if live(g):
                    top_of(top3, pair[:, 1, 0:N], bcast3_s, top3_s, g, 1)
                    negative_max(g, top3, att3[:, 1:2], ntop3, nmax3, top3_s, ntop3_s, nmax3_s, p3_s, 1)
                    dve.tensor_scalar(z3[:, :], pair[:, 1, 0:N], att3[:, 1:2], None, ALU.add).then_inc(z3_s, 1)
                    wait(dve, z3_s, g)
                    wait(dve, p3_s, g - 1)
                    dve.scalar_tensor_tensor(out=e3[:, :], in0=z3[:, :], scalar=SLOPE, in1=z3[:, :],
                                             op0=ALU.mult, op1=ALU.max).then_inc(e3_s, 1)

            def residual2(g, c):
                if live(g):
                    wait(dve, av2_s, g)
                    wait(dve, x_b2_s, g)
                    dve.scalar_tensor_tensor(out=y2[:, :], in0=pair[:, 0, :], scalar=rden2[:, 0:1],
                                             in1=x_b2[:, c, :], op0=ALU.mult, op1=ALU.add).then_inc(y2_s, 1)
                    moments(g, ln2, y2, y2_s, bn2_s, mv2_s, ve2_s)

            def moments(g, ln, y, y_s, bn_s, mv_s, ve_s):
                wait(dve, y_s, g)
                dve.bn_stats(ln[:, 0:6], y[:, :]).then_inc(bn_s, 1)
                dve.wait_ge(bias_in, 2 * 16)
                wait(dve, bn_s, g)
                dve.bn_aggr(ln[:, 6:8], ln[:, 0:6]).then_inc(mv_s, 1)
                wait(dve, mv_s, g)
                dve.tensor_scalar(ln[:, 8:9], ln[:, 7:8], EPS, None, ALU.add).then_inc(ve_s, 1)

            def refine_root(g, ln, guess_s, step_s, factor_s, rstd_s):
                wait(dve, guess_s, g)
                dve.scalar_tensor_tensor(out=ln[:, 11:12], in0=ln[:, 10:11], scalar=ln[:, 10:11], in1=ln[:, 8:9],
                                         op0=ALU.mult, op1=ALU.mult).then_inc(step_s, 1)
                wait(dve, step_s, g)
                dve.tensor_scalar(ln[:, 12:13], ln[:, 11:12], -0.5, 1.5, ALU.mult, ALU.add).then_inc(factor_s, 1)
                wait(dve, factor_s, g)
                dve.tensor_tensor(ln[:, 13:14], ln[:, 12:13], ln[:, 10:11], ALU.mult).then_inc(rstd_s, 1)
                wait(dve, rstd_s, g)

            def normalise2(g, c):
                if live(g):
                    refine_root(g, ln2, guess2_s, step2_s, factor2_s, rstd2_s)
                    wait(dve, x1_relu3_s, g - 2)
                    dve.tensor_scalar(x1[:, c, :], y2[:, :], ln2[:, 6:7], ln2[:, 13:14],
                                      ALU.subtract, ALU.mult).then_inc(x1_s, 1)

            def p3_rest(g):
                if live(g):
                    wait(dve, p3_s, g)
                    wait(dve, p3_hi_s, g - 1)
                    dve.reciprocal(rden3[:, :], den3[:, :]).then_inc(rden3_s, 1)
                    wait(dve, p3_hi_s, g)
                    wait(dve, av3_s, g - 1)
                    dve.scalar_tensor_tensor(out=p3_lo[:, :], in0=p3[:, :], scalar=rden3[:, 0:1], in1=p3_hi[:, :],
                                             op0=ALU.mult, op1=ALU.subtract).then_inc(p3_lo_s, 1)

            def x1_rest(g):
                if live(g):
                    wait(dve, x1_hi_s, g)
                    wait(dve, xw3_s, g - 1)
                    dve.tensor_tensor(x1_lo[:, :], pair[:, 1, :], x1_hi[:, :], ALU.subtract).then_inc(x1_lo_s, 1)

            def ht_rest(g):
                if live(g):
                    for half in range(2):
                        cols = slice(half * 512, (half + 1) * 512)
                        wait(dve, ht_hi_s, g, 2, 1 - half)
                        wait(dve, hw2_s, g - 1)
                        dve.tensor_tensor(ht_lo[:, cols], heads[:, half, :], ht_hi[:, cols],
                                          ALU.subtract).then_inc(ht_lo_s, 1)

            def residual3(g):
                if live(g):
                    wait(dve, x1_relu3_s, g)
                    dve.scalar_tensor_tensor(out=y3[:, :], in0=pair[:, 0, :], scalar=SLOPE, in1=x1_relu3[:, :],
                                             op0=ALU.mult, op1=ALU.add).then_inc(y3_s, 1)
                    moments(g, ln3, y3, y3_s, bn3_s, mv3_s, ve3_s)

            def normalise3(g, c):
                if live(g):
                    refine_root(g, ln3, guess3_s, step3_s, factor3_s, rstd3_s)
                    wait_dma(dve, res_out, g - 2, c)
                    dve.tensor_scalar(res[:, c, :], y3[:, :], ln3[:, 6:7], ln3[:, 13:14],
                                      ALU.subtract, ALU.mult).then_inc(res_s, 1)

            def evacuate1(g):
                if live(g):
                    wait(dve, xw1_s, g)
                    wait(dve, bcast1_s, g - 1)
                    dve.tensor_copy(att1[:, :], wide[:, 2, S1:S1 + 2 * H]).then_inc(att1_s, 1)
                    wait(dve, xl_hi_s, g - 1)
                    wait(dve, xl_lo_s, g - 1)
                    dve.tensor_tensor(xl[:, :].rearrange("p (a b) -> p a b", a=3), wide[:, :, 0:C1P],
                                      b1_rows[:, :].rearrange("p (a b) -> p a b", a=3),
                                      ALU.add).then_inc(xl_s, 1)

            def scores1(g):
                if live(g):
                    top_of(top1, score[:, :].rearrange("p (k s) -> p k s", k=H), bcast1_s, top1_s, g, H)
                    wait(dve, att1_s, g)
                    wait(dve, e1_s, g - 1)
                    dve.tensor_tensor(z1[:, :, :], score[:, :].rearrange("p (k s) -> p k s", k=H),
                                      att1[:, H:2 * H].unsqueeze(2).broadcast_to([P, H, N]),
                                      ALU.add).then_inc(z1_s, 1)
                    negative_max(g, top1, att1[:, H:2 * H], ntop1, nmax1, top1_s, ntop1_s, nmax1_s, p1_s, H)
                    wait(dve, z1_s, g)
                    wait(dve, p1_s, g - 1, H)
                    dve.scalar_tensor_tensor(out=e1[:, :, :], in0=z1[:, :, :], scalar=SLOPE, in1=z1[:, :, :],
                                             op0=ALU.mult, op1=ALU.max).then_inc(e1_s, 1)

            def denominators1(g):
                if live(g):
                    wait(dve, p1_s, g, H)
                    dve.reciprocal(rden1[:, :], den1[:, :]).then_inc(rden1_s, 1)

            def att_h(g):
                if live(g):
                    wait(dve, hw2_s, g)
                    dve.tensor_copy(att2[:, :], pair[:, 1, S2:S2 + 2]).then_inc(att2_s, 1)

            def x2_rest(g):
                if live(g):
                    wait(dve, x2_hi_s, g)
                    wait(dve, av2_s, g - 1)
                    dve.tensor_tensor(x2_lo[:, :].rearrange("p (a b) -> p a b", a=2), pair[:, :, 0:C2P],
                                      x2_hi[:, :].rearrange("p (a b) -> p a b", a=2),
                                      ALU.subtract).then_inc(x2_lo_s, 1)

            def p1_rest(g):
                if live(g):
                    wait(dve, p1_hi_s, g)
                    wait(dve, av1_s, g - 1, 2)
                    dve.tensor_tensor(p1_lo[:, :, :].rearrange("p a b -> p (a b)"), score[:, :],
                                      p1_hi[:, :, :].rearrange("p a b -> p (a b)"),
                                      ALU.subtract).then_inc(p1_lo_s, 1)

            def scores2(g):
                if live(g):
                    top_of(top2, score[:, 0:N], bcast2_s, top2_s, g, 1)
                    negative_max(g, top2, att2[:, 1:2], ntop2, nmax2, top2_s, ntop2_s, nmax2_s, p2_s, 1)
                    dve.tensor_scalar(z2[:, :], score[:, 0:N], att2[:, 1:2], None, ALU.add).then_inc(z2_s, 1)
                    wait(dve, z2_s, g)
                    wait(dve, p2_s, g - 1)
                    dve.scalar_tensor_tensor(out=e2[:, :], in0=z2[:, :], scalar=SLOPE, in1=z2[:, :],
                                             op0=ALU.mult, op1=ALU.max).then_inc(e2_s, 1)

            def p2_rest(g):
                if live(g):
                    wait(dve, p2_s, g)
                    dve.reciprocal(rden2[:, :], den2[:, :]).then_inc(rden2_s, 1)
                    wait(dve, p2_hi_s, g)
                    wait(dve, av2_s, g - 1)
                    dve.tensor_tensor(p2_lo[:, :], score[:, 0:N], p2_hi[:, :], ALU.subtract).then_inc(p2_lo_s, 1)

            def step(i, c):
                if isinstance(i, int) and i == 0:
                    make_mask_t(0, 0)
                att_wh(i - 3)
                wh_rest(i - 3)
                residual2(i - 2, c)
                elu(i - 1)
                scores3(i - 3)
                normalise2(i - 2, c)
                p3_rest(i - 3)
                x1_rest(i - 2)
                ht_rest(i - 1)
                make_mask1(i - 1, 1 - c)
                residual3(i - 3)
                evacuate1(i)
                scores1(i)
                make_mask_t(i + 1, 1 - c)
                normalise3(i - 3, 1 - c)
                denominators1(i)
                att_h(i - 1)
                x2_rest(i - 1)
                p1_rest(i)
                scores2(i - 1)
                p2_rest(i - 1)

            run(dve, step)

        @block.gpsimd
        def _(pool):
            pool.memset(ident[:, :], 0.0).then_inc(ident_zero, 1)
            pool.wait_ge(ident_zero, 1)
            pool.affine_select(out=ident[:, :], in_=ident[:, :], compare_op=ALU.not_equal, fill=1.0, base=0,
                               pattern=[[-1, P]], channel_multiplier=1).then_inc(ident_made, 1)
            pool.wait_ge(ident_made, 1)
            pool.tensor_copy(ident_b[:, :], ident[:, :])
            pool.tensor_scalar(not_eye[:, :], ident[:, :], -1.0, 1.0, ALU.mult, ALU.add).then_inc(consts_made, 1)
            for t, (_n, kt, cols, hi, lo, _src) in enumerate(weight_tiles()):
                pool.wait_ge(w_hi_made, t + 1)
                pool.tensor_tensor(lo, w_raw[:, t % 2, 0:cols], hi, ALU.subtract).then_inc(w_lo_made, 1)
            pool.wait_ge(consts_made, 1)
            pool.wait_ge(bias_in, 2 * 16)

            def residual_bias(g, c):
                if live(g):
                    wait_dma(pool, x_in_s, g, c)
                    wait(pool, y2_s, g - 2)
                    pool.tensor_tensor(x_b2[:, c, :], x_in[:, c, :], b2_rows[:, :], ALU.add).then_inc(x_b2_s, 1)

            def residual_relu(g, c):
                if live(g):
                    wait(pool, relu3_s, g)
                    wait(pool, x1_s, g)
                    wait(pool, y3_s, g - 1)
                    pool.tensor_tensor(x1_relu3[:, :], x1[:, c, :], relu3[:, :], ALU.add).then_inc(x1_relu3_s, 1)

            def make_mask0(g, c):
                if live(g):
                    wait(pool, mask_t_s, g)
                    wait(pool, bcast2_s, g - 2)
                    pool.tensor_tensor(mask0[:, c, :], mask_t[:, :], not_eye[:, :], ALU.mult).then_inc(mask0_s, 1)

            def xl_rest(g):
                if live(g):
                    wait(pool, xl_hi_s, g)
                    wait(pool, av1_s, g - 1, 2)
                    pool.tensor_tensor(xl_lo[:, :], xl[:, 0:HF], xl_hi[:, :], ALU.subtract).then_inc(xl_lo_s, 1)

            def xt_rest(g, c):
                if live(g):
                    wait(pool, xt_hi_s, g)
                    wait(pool, xw1_s, g - 2)
                    pool.tensor_tensor(xt_lo[:, c, :], xt[:, c, :], xt_hi[:, c, :], ALU.subtract).then_inc(xt_lo_s, 1)

            def step(i, c):
                if isinstance(i, int) and i == 0:
                    make_mask0(0, 0)
                    xt_rest(0, 0)
                residual_bias(i - 1, 1 - c)
                residual_relu(i - 3, 1 - c)
                xl_rest(i)
                xt_rest(i + 1, 1 - c)
                make_mask0(i + 1, 1 - c)

            run(pool, step)


def kernel(x, adj, L0_gnn_W1, L0_gnn_att_src1, L0_gnn_att_dst1, L0_gnn_b1, L0_gnn_W2, L0_gnn_att_src2,
           L0_gnn_att_dst2, L0_gnn_b2, L1_gnn_W, L1_gnn_a):
    import numpy as np
    import concourse.bacc as bacc
    from concourse.bass_utils import run_bass_kernel_spmd

    x, adj = np.asarray(x), np.asarray(adj)
    B, N, D = x.shape
    given = {
        "x": x,
        "x_t": x.reshape(B, N, D // P, P).transpose(0, 3, 2, 1).reshape(B, P, D),
        "adj_t": adj.transpose(0, 2, 1),
        "w1": L0_gnn_W1, "a_src1": L0_gnn_att_src1, "a_dst1": L0_gnn_att_dst1, "b1": L0_gnn_b1,
        "w2": L0_gnn_W2, "a_src2": L0_gnn_att_src2, "a_dst2": L0_gnn_att_dst2, "b2": L0_gnn_b2,
        "w3": L1_gnn_W, "a3": L1_gnn_a,
    }
    nc = bacc.Bacc("TRN2", target_bir_lowering=False, num_devices=1)
    arrays, args = {}, {}
    for name, a in given.items():
        a = np.ascontiguousarray(a)
        arrays[f"in_{name}"] = a
        args[name] = nc.dram_tensor(f"in_{name}", a.shape, mybir.dt.from_np(a.dtype), kind="ExternalInput").ap()
    args["out"] = nc.dram_tensor("out", (B, N, D), F32, kind="ExternalOutput").ap()
    resnorm_gat_kernel(nc, **args)
    r = run_bass_kernel_spmd(nc, [arrays], core_ids=[0])
    return r.results[0]["out"]
```

```python
from contextlib import ExitStack

import concourse.bass as bass
from concourse import mybir

F32 = mybir.dt.float32
F32R = mybir.dt.float32r
BF16 = mybir.dt.bfloat16
I32 = mybir.dt.int32
ALU = mybir.AluOpType
ACT = mybir.ActivationFunctionType
AX = mybir.AxisListType

P = 128
MASKED = -9e15
SLOPE = 0.2
EPS = 1e-5


def resnorm_gat_kernel(nc, x, x_t, adj_t, w1, a_src1, a_dst1, b1, w2, a_src2, a_dst2, b2, w3, a3, out):
    B, N, D = x.shape
    H, F = a_src1.shape
    HF = H * F
    assert N == P and D % P == 0 and F == 256 and D == 512
    KT1, KT2, KT3 = D // P, HF // P, D // P
    C1 = HF + 2 * H
    C1P = C1 // 3
    C2 = D + 4
    C2P = C2 // 2
    S1 = HF - 2 * C1P
    S2 = D - C2P

    LOOP_FROM, LOOP_TO, STEPS = 6, B - 4, B + 4

    with ExitStack() as ctx:
        def sb(name, shape, dt=F32):
            return ctx.enter_context(nc.sbuf_tensor(name, shape, dt))

        def sem(name):
            return ctx.enter_context(nc.semaphore(name))

        ident = sb("ident", [P, P])
        ident_b = sb("ident_b", [P, P], BF16)
        not_eye = sb("not_eye", [P, P], BF16)
        w1_hi, w1_lo = sb("w1_hi", [P, KT1, C1], F32R), sb("w1_lo", [P, KT1, C1], F32R)
        w2_hi, w2_lo = sb("w2_hi", [P, KT2, C2], F32R), sb("w2_lo", [P, KT2, C2], F32R)
        w3_hi, w3_lo = sb("w3_hi", [P, KT3, C2], F32R), sb("w3_lo", [P, KT3, C2], F32R)
        b1_rows = sb("b1_rows", [P, C1])
        b2_rows = sb("b2_rows", [P, D])
        w_raw = sb("w_raw", [P, 2, C1])

        xt = sb("xt", [P, 2, D])
        xt_hi, xt_lo = sb("xt_hi", [P, 2, D], F32R), sb("xt_lo", [P, 2, D], F32R)
        x_in, x_b2 = sb("x_in", [P, 2, D]), sb("x_b2", [P, 2, D])
        adj = sb("adj", [P, 2, N], I32)
        mask0, mask1 = sb("mask0", [P, 2, N], BF16), sb("mask1", [P, 2, N], BF16)
        mask_t = sb("mask_t", [P, N], BF16)
        att1, att2, att3 = sb("att1", [P, 2 * H]), sb("att2", [P, 2]), sb("att3", [P, 2])
        xl = sb("xl", [P, C1])
        xl_hi, xl_lo = sb("xl_hi", [P, HF], F32R), sb("xl_lo", [P, HF], F32R)
        z1, e1, p1 = sb("z1", [P, H, N]), sb("e1", [P, H, N]), sb("p1", [P, H, N])
        p1_hi, p1_lo = sb("p1_hi", [P, H, N], F32R), sb("p1_lo", [P, H, N], F32R)
        top1, ntop1, nmax1 = sb("top1", [P, H]), sb("ntop1", [P, H]), sb("nmax1", [P, H])
        den1, rden1 = sb("den1", [P, H]), sb("rden1", [P, H])
        p1_n = sb("p1_n", [P, H, N])
        neg, ex, h = sb("neg", [P, HF]), sb("ex", [P, HF]), sb("h", [P, HF])
        ht_hi, ht_lo = sb("ht_hi", [P, HF], F32R), sb("ht_lo", [P, HF], F32R)
        x2 = sb("x2", [P, C2])
        x2_hi, x2_lo = sb("x2_hi", [P, C2], F32R), sb("x2_lo", [P, C2], F32R)
        z2, e2, p2 = sb("z2", [P, N]), sb("e2", [P, N]), sb("p2", [P, N])
        p2_hi, p2_lo = sb("p2_hi", [P, N], F32R), sb("p2_lo", [P, N], F32R)
        top2, ntop2, nmax2 = sb("top2", [P, 1]), sb("ntop2", [P, 1]), sb("nmax2", [P, 1])
        den2, rden2 = sb("den2", [P, 1]), sb("rden2", [P, 1])
        y2, x1 = sb("y2", [P, D]), sb("x1", [P, 2, D])
        x1_hi, x1_lo = sb("x1_hi", [P, D], F32R), sb("x1_lo", [P, D], F32R)
        wh = sb("wh", [P, C2])
        wh_hi, wh_lo = sb("wh_hi", [P, C2], F32R), sb("wh_lo", [P, C2], F32R)
        z3, e3, p3 = sb("z3", [P, N]), sb("e3", [P, N]), sb("p3", [P, N])
        p3_hi, p3_lo = sb("p3_hi", [P, N], F32R), sb("p3_lo", [P, N], F32R)
        top3, ntop3, nmax3 = sb("top3", [P, 1]), sb("ntop3", [P, 1]), sb("nmax3", [P, 1])
        den3, rden3 = sb("den3", [P, 1]), sb("rden3", [P, 1])
        relu3, x1_relu3, y3 = sb("relu3", [P, D]), sb("x1_relu3", [P, D]), sb("y3", [P, D])
        res = sb("res", [P, 2, D])
        ln2, ln3 = sb("ln2", [P, 16]), sb("ln3", [P, 16])

        wide = ctx.enter_context(nc.psum_tensor("wide", [P, 3, 512], F32))
        pair = ctx.enter_context(nc.psum_tensor("pair", [P, 2, 512], F32))
        heads = ctx.enter_context(nc.psum_tensor("heads", [P, 2, 512], F32))
        score = ctx.enter_context(nc.psum_tensor("score", [P, 512], F32))

        vectors_in, bias_in = sem("vectors_in"), sem("bias_in")
        raw_in, xt_in, x_in_s, adj_in, res_out = (
            [sem(f"{n}_{c}") for c in range(2)] for n in ("raw_in", "xt_in", "x_in_s", "adj_in", "res_out"))
        ident_zero, ident_made, consts_made = sem("ident_zero"), sem("ident_made"), sem("consts_made")
        raw_pads, product_used, raw_att, w_hi_made, w_lo_made = sem("raw_pads"), sem("product_used"), sem("raw_att"), sem("w_hi_made"), sem("w_lo_made")
        (xt_hi_s, xt_lo_s, x_b2_s, mask_t_s, mask0_s, mask1_s) = map(
            sem, ("xt_hi_s", "xt_lo_s", "x_b2_s", "mask_t_s", "mask0_s", "mask1_s"))
        (xw1_s, bcast1_s, pt1_s, av1_s, ht_s) = map(sem, ("xw1_s", "bcast1_s", "pt1_s", "av1_s", "ht_s"))
        (hw2_s, bcast2_s, pt2_s, av2_s, x1t_s) = map(sem, ("hw2_s", "bcast2_s", "pt2_s", "av2_s", "x1t_s"))
        (xw3_s, bcast3_s, av3_s) = map(sem, ("xw3_s", "bcast3_s", "av3_s"))
        (att1_s, xl_s, xl_hi_s, xl_lo_s) = map(sem, ("att1_s", "xl_s", "xl_hi_s", "xl_lo_s"))
        (top1_s, ntop1_s, nmax1_s, z1_s, e1_s, p1_s, rden1_s, p1_hi_s, p1_lo_s) = map(
            sem, ("top1_s", "ntop1_s", "nmax1_s", "z1_s", "e1_s", "p1_s", "rden1_s", "p1_hi_s", "p1_lo_s"))
        (p1_n_s, neg_s, ex_s, h_s, ht_hi_s, ht_lo_s) = map(sem, ("p1_n_s", "neg_s", "ex_s", "h_s", "ht_hi_s", "ht_lo_s"))
        x2_s, wh_s = sem("x2_s"), sem("wh_s")
        (att2_s, x2_hi_s, x2_lo_s, top2_s, ntop2_s, nmax2_s, z2_s, e2_s, p2_s, rden2_s, p2_hi_s, p2_lo_s) = map(
            sem, ("att2_s", "x2_hi_s", "x2_lo_s", "top2_s", "ntop2_s", "nmax2_s", "z2_s", "e2_s", "p2_s",
                  "rden2_s", "p2_hi_s", "p2_lo_s"))
        (y2_s, bn2_s, mv2_s, ve2_s, lnv2_s, guess2_s, step2_s, factor2_s, rstd2_s, x1_s, x1_hi_s, x1_lo_s) = map(
            sem, ("y2_s", "bn2_s", "mv2_s", "ve2_s", "lnv2_s", "guess2_s", "step2_s", "factor2_s", "rstd2_s",
                  "x1_s", "x1_hi_s", "x1_lo_s"))
        (att3_s, wh_hi_s, wh_lo_s, top3_s, ntop3_s, nmax3_s, z3_s, e3_s, p3_s, rden3_s, p3_hi_s, p3_lo_s) = map(
            sem, ("att3_s", "wh_hi_s", "wh_lo_s", "top3_s", "ntop3_s", "nmax3_s", "z3_s", "e3_s", "p3_s",
                  "rden3_s", "p3_hi_s", "p3_lo_s"))
        (relu3_s, x1_relu3_s, y3_s, bn3_s, mv3_s, ve3_s, lnv3_s, guess3_s, step3_s, factor3_s, rstd3_s, res_s) = map(
            sem, ("relu3_s", "x1_relu3_s", "y3_s", "bn3_s", "mv3_s", "ve3_s", "lnv3_s", "guess3_s", "step3_s",
                  "factor3_s", "rstd3_s", "res_s"))

        def live(g):
            return not isinstance(g, int) or 0 <= g < B

        def wait(eng, s, g, per=1, short=0):
            if not isinstance(g, int) or g >= 0:
                eng.wait_ge(s, g * per + (per - short))

        def wait_dma(eng, s, g, c):
            if not isinstance(g, int) or g >= 0:
                eng.wait_ge(s[c], 8 * g + (16 - 8 * c))

        def run(eng, step):
            for i in range(LOOP_FROM):
                step(i, i % 2)
            with eng.Fori(LOOP_FROM, LOOP_TO, 2) as i:
                step(i, 0)
                step(i + 1, 1)
            for i in range(LOOP_TO, STEPS):
                step(i, i % 2)

        def weight_tiles():
            for kt in range(KT1):
                yield "w1", kt, C1, w1_hi[:, kt, :], w1_lo[:, kt, :], w1
            for kt in range(KT2):
                yield "w2", kt, C2, w2_hi[:, kt, :], w2_lo[:, kt, :], w2
            for kt in range(KT3):
                yield "w3", kt, C2, w3_hi[:, kt, :], w3_lo[:, kt, :], w3
        TILES = KT1 + KT2 + KT3
        a_src1_rows, a_dst1_rows = h, neg
        a2_rows, a3_rows = res, x1

        block = ctx.enter_context(nc.Block())

        @block.sync
        def _(sp):
            def rows(v, n):
                return v.unsqueeze(0).broadcast_to([P, n])
            sp.dma_start(a_src1_rows[:, :], rows(a_src1.rearrange("h f -> (h f)"), HF)).then_inc(vectors_in, 16)
            sp.dma_start(a_dst1_rows[:, :], rows(a_dst1.rearrange("h f -> (h f)"), HF)).then_inc(vectors_in, 16)
            sp.dma_start(a2_rows[:, 0, :], rows(a_src2.rearrange("h f -> (h f)"), D)).then_inc(vectors_in, 16)
            sp.dma_start(a2_rows[:, 1, :], rows(a_dst2.rearrange("h f -> (h f)"), D)).then_inc(vectors_in, 16)
            sp.dma_start(a3_rows[:, :, :].rearrange("p a b -> p (a b)"), rows(a3.rearrange("f o -> (f o)"), 2 * D)).then_inc(vectors_in, 16)
            for t, (_n, kt, cols, _hi, _lo, src) in enumerate(weight_tiles()):
                if t >= 2:
                    sp.wait_ge(w_hi_made, t - 1)
                    sp.wait_ge(w_lo_made, t - 1)
                n = src.shape[1]
                sp.dma_start(w_raw[:, t % 2, 0:n], src[kt * P:(kt + 1) * P, :]).then_inc(raw_in[t % 2], 16)
                if t == 1:
                    sp.dma_start(b1_rows[:, 0:HF], rows(b1, HF)).then_inc(bias_in, 16)
                    sp.dma_start(b2_rows[:, :], rows(b2, D)).then_inc(bias_in, 16)

            def load_xt(g, c):
                if live(g):
                    wait(sp, xt_hi_s, g - 2)
                    wait(sp, xt_lo_s, g - 2)
                    sp.dma_start(xt[:, c, :], x_t[g]).then_inc(xt_in[c], 16)

            def load_x(g, c):
                if live(g):
                    wait(sp, x_b2_s, g - 2)
                    sp.dma_start(x_in[:, c, :], x[g]).then_inc(x_in_s[c], 16)

            def load_adj(g, c):
                if live(g):
                    wait(sp, mask_t_s, g - 2)
                    wait(sp, mask1_s, g - 2)
                    sp.dma_start(adj[:, c, :], adj_t[g]).then_inc(adj_in[c], 16)

            def step(i, c):
                if isinstance(i, int) and i == 0:
                    for g in range(2):
                        load_xt(g, g)
                    load_adj(0, 0)
                load_x(i, c)
                load_xt(i + 2, c)
                load_adj(i + 1, 1 - c)
                g = i - 4
                if live(g):
                    wait(sp, res_s, g)
                    sp.dma_start(out[g], res[:, c, :]).then_inc(res_out[c], 16)

            run(sp, step)
            for c in range(2):
                sp.wait_ge(res_out[c], 16 * (B // 2))

        @block.tensor
        def _(pe):
            pe.wait_ge(consts_made, 1)

            def split_matmul(dst, k, kts, lhs, rhs, last=None):
                n = 0
                for a, b in ((0, 0), (0, 1), (1, 0)):
                    for ch, d in enumerate(dst):
                        mm = pe.matmul(d, lhs[a], rhs[b](ch), start=(k == 0 and n == 0),
                                       stop=(k == kts - 1 and n == 2), skip_group_check=True)
                    n += 1
                return mm

            def xw1(g, c, kts):
                if not live(g):
                    return
                if kts[0] == 0:
                    if isinstance(g, int) and g == 0:
                        pe.wait_ge(w_hi_made, KT1)
                        pe.wait_ge(w_lo_made, KT1)
                    wait(pe, xt_hi_s, g)
                    wait(pe, xt_lo_s, g)
                    wait(pe, wh_s, g - 3)
                    wait(pe, p2_lo_s, g - 2)
                for k in kts:
                    mm = split_matmul(
                        [wide[:, ch, 0:C1P] for ch in range(3)], k, KT1,
                        (xt_hi[:, c, k * P:(k + 1) * P], xt_lo[:, c, k * P:(k + 1) * P]),
                        (lambda ch: w1_hi[:, k, ch * C1P:(ch + 1) * C1P],
                         lambda ch: w1_lo[:, k, ch * C1P:(ch + 1) * C1P]))
                if kts[-1] == KT1 - 1:
                    mm.then_inc(xw1_s, 1)

            def hw2(g, kts):
                if not live(g):
                    return
                if kts[0] == 0:
                    if isinstance(g, int) and g == 0:
                        pe.wait_ge(w_hi_made, KT1 + KT2)
                        pe.wait_ge(w_lo_made, KT1 + KT2)
                    wait(pe, y2_s, g - 1)
                    wait(pe, z3_s, g - 2)
                    wait(pe, top3_s, g - 2)
                for k in kts:
                    if k in (0, KT2 // 2):
                        half = 1 if k == 0 else 0
                        wait(pe, ht_hi_s, g, 2, half)
                        wait(pe, ht_lo_s, g, 2, half)
                    mm = split_matmul(
                        [pair[:, ch, 0:C2P] for ch in range(2)], k, KT2,
                        (ht_hi[:, k * P:(k + 1) * P], ht_lo[:, k * P:(k + 1) * P]),
                        (lambda ch: w2_hi[:, k, ch * C2P:(ch + 1) * C2P],
                         lambda ch: w2_lo[:, k, ch * C2P:(ch + 1) * C2P]))
                if kts[-1] == KT2 - 1:
                    mm.then_inc(hw2_s, 1)

            def xw3(g, kts):
                if not live(g):
                    return
                if kts[0] == 0:
                    if isinstance(g, int) and g == 0:
                        pe.wait_ge(w_hi_made, TILES)
                        pe.wait_ge(w_lo_made, TILES)
                    wait(pe, x1_hi_s, g)
                    wait(pe, x1_lo_s, g)
                    if not isinstance(g, int) or g + 2 < B:
                        wait(pe, xl_s, g + 2)
                for k in kts:
                    mm = split_matmul(
                        [wide[:, ch, 0:C2P] for ch in range(2)], k, KT3,
                        (x1_hi[:, k * P:(k + 1) * P], x1_lo[:, k * P:(k + 1) * P]),
                        (lambda ch: w3_hi[:, k, ch * C2P:(ch + 1) * C2P],
                         lambda ch: w3_lo[:, k, ch * C2P:(ch + 1) * C2P]))
                if kts[-1] == KT3 - 1:
                    mm.then_inc(xw3_s, 1)

            def spread(dst, col, mask, n, done):
                for k in range(n):
                    pe.matmul(dst[:, k * N:(k + 1) * N], col[:, k:k + 1].broadcast_to([P, P]), ident[:, :],
                              is_transpose=True, start=(k == 0), stop=False, skip_group_check=True)
                pe.matmul(dst[:, 0:n * N].rearrange("p (k s) -> p k s", k=n), ident_b[:, :],
                          mask.unsqueeze(1).broadcast_to([P, n, N]), start=False, stop=True,
                          skip_group_check=True).then_inc(done, 1)

            def bcast1(g, c):
                if live(g):
                    wait(pe, att1_s, g)
                    wait(pe, mask0_s, g)
                    wait(pe, p1_lo_s, g - 1)
                    spread(score, att1, mask0[:, c, :], H, bcast1_s)

            def bcast2(g, c):
                if live(g):
                    wait(pe, att2_s, g)
                    wait(pe, x1_lo_s, g - 1)
                    spread(wide[:, 2, :], att2, mask0[:, c, :], 1, bcast2_s)

            def bcast3(g, c):
                if live(g):
                    wait(pe, att3_s, g)
                    wait(pe, mask1_s, g)
                    spread(pair[:, 1, :], att3, mask1[:, c, :], 1, bcast3_s)

            def pt1(g):
                if live(g):
                    wait(pe, p1_n_s, g)
                    for k in range(H):
                        mm = pe.transpose(score[:, k * N:(k + 1) * N], p1_n[:, k, :], ident[:, :])
                    mm.then_inc(pt1_s, 1)

            def pt2(g):
                if live(g):
                    wait(pe, p2_s, g)
                    pe.transpose(wide[:, 2, 0:N], p2[:, :], ident[:, :]).then_inc(pt2_s, 1)

            def av1(g):
                if live(g):
                    wait(pe, p1_hi_s, g)
                    wait(pe, xl_hi_s, g)
                    wait(pe, xl_lo_s, g)
                    wait(pe, y3_s, g - 3)
                    for k in range(H):
                        for n, v in enumerate((xl_hi, xl_lo)):
                            pe.matmul(heads[:, k // 2, (k % 2) * F:(k % 2 + 1) * F], p1_hi[:, k, :],
                                      v[:, k * F:(k + 1) * F], start=(k % 2 == 0 and n == 0), stop=False,
                                      skip_group_check=True)
                    wait(pe, p1_lo_s, g)
                    for k in range(H):
                        mm = pe.matmul(heads[:, k // 2, (k % 2) * F:(k % 2 + 1) * F], p1_lo[:, k, :],
                                       xl_hi[:, k * F:(k + 1) * F], start=False, stop=(k % 2 == 1),
                                       skip_group_check=True)
                        if k % 2 == 1:
                            mm.then_inc(av1_s, 1)

            def ht(g):
                if live(g):
                    for half in range(2):
                        wait(pe, h_s, g, 2, 0)
                        for k in range(4):
                            f = half * 4 + k
                            mm = pe.transpose(heads[:, half, k * P:(k + 1) * P], h[:, f * P:(f + 1) * P],
                                              ident[:, :])
                        mm.then_inc(ht_s, 1)

            def av_wide(dst, p_hi, p_lo, v_hi, v_lo, done):
                for n, (a, b) in enumerate(((p_hi, v_hi), (p_hi, v_lo), (p_lo, v_hi))):
                    mm = pe.matmul(dst, a[:, :], b[:, 0:D], start=(n == 0), stop=(n == 2))
                mm.then_inc(done, 1)

            def av2(g):
                if live(g):
                    wait(pe, p2_hi_s, g)
                    wait(pe, p2_lo_s, g)
                    wait(pe, x2_hi_s, g)
                    wait(pe, x2_lo_s, g)
                    av_wide(pair[:, 0, :], p2_hi, p2_lo, x2_hi, x2_lo, av2_s)

            def x1t(g, c):
                if live(g):
                    wait(pe, x1_s, g)
                    if not isinstance(g, int) or g + 2 < B:
                        wait(pe, xl_s, g + 2)
                    for k in range(KT3):
                        mm = pe.transpose(wide[:, 2, k * P:(k + 1) * P], x1[:, c, k * P:(k + 1) * P],
                                          ident[:, :])
                    mm.then_inc(x1t_s, 1)

            def av3(g):
                if live(g):
                    wait(pe, p3_hi_s, g)
                    wait(pe, p3_lo_s, g)
                    wait(pe, wh_hi_s, g)
                    wait(pe, wh_lo_s, g)
                    if not isinstance(g, int) or g + 2 < B:
                        wait(pe, ht_lo_s, g + 2, 2)
                    av_wide(heads[:, 0, :], p3_hi, p3_lo, wh_hi, wh_lo, av3_s)

            def step(i, c):
                xw1(i, c, [0])
                bcast3(i - 3, 1 - c)
                xw1(i, c, [1])
                ht(i - 1)
                xw1(i, c, [2, 3])
                hw2(i - 1, [0, 1])
                bcast1(i, c)
                av3(i - 3)
                hw2(i - 1, [2])
                x1t(i - 2, c)
                hw2(i - 1, [3, 4, 5, 6, 7])
                xw3(i - 2, [0])
                bcast2(i - 1, 1 - c)
                xw3(i - 2, [1])
                pt1(i)
                xw3(i - 2, [2, 3])
                pt2(i - 1)
                av1(i)
                av2(i - 1)

            run(pe, step)

        @block.scalar
        def _(act):
            act.preload_act_table_set("natural_log_exp_and_others")
            for t, (_n, kt, cols, hi, _lo, _src) in enumerate(weight_tiles()):
                act.wait_ge(raw_att, t + 1)
                act.activation(hi, w_raw[:, t % 2, 0:cols], ACT.Copy).then_inc(w_hi_made, 1)

            def wh_copy(g):
                if live(g):
                    wait(act, att3_s, g)
                    wait(act, wh_lo_s, g - 1)
                    wait(act, wh_hi_s, g - 1)
                    act.activation(wh[:, :].rearrange("p (a b) -> p a b", a=2), wide[:, 0:2, 0:C2P],
                                   ACT.Copy).then_inc(wh_s, 1)

            def wh_halves(g):
                if live(g):
                    wait(act, wh_s, g)
                    wait(act, av3_s, g - 1)
                    act.activation(wh_hi[:, :], wh[:, :], ACT.Copy).then_inc(wh_hi_s, 1)

            def exp3(g):
                if live(g):
                    wait(act, e3_s, g)
                    wait(act, nmax3_s, g)
                    wait(act, p3_lo_s, g - 1)
                    wait(act, rden3_s, g - 1)
                    act.activation(p3[:, :], e3[:, :], ACT.Exp, bias=nmax3[:, 0:1],
                                   accum_out=den3[:, 0:1]).then_inc(p3_s, 1)
                    wait(act, rden3_s, g)
                    wait(act, av3_s, g - 1)
                    act.activation(p3_hi[:, :], p3[:, :], ACT.Copy, scale=rden3[:, 0:1]).then_inc(p3_hi_s, 1)

            def x1_halves(g):
                if live(g):
                    wait(act, x1t_s, g)
                    wait(act, xw3_s, g - 1)
                    act.activation(x1_hi[:, :], wide[:, 2, :], ACT.Copy).then_inc(x1_hi_s, 1)

            def ht_halves(g):
                if live(g):
                    for half in range(2):
                        wait(act, ht_s, g, 2, 1 - half)
                        wait(act, hw2_s, g - 1)
                        act.activation(ht_hi[:, half * 512:(half + 1) * 512], heads[:, half, :],
                                       ACT.Copy, bias=-1.0).then_inc(ht_hi_s, 1)

            def xt_halves(g, c):
                if live(g):
                    wait_dma(act, xt_in, g, c)
                    wait(act, xw1_s, g - 2)
                    act.activation(xt_hi[:, c, :], xt[:, c, :], ACT.Copy).then_inc(xt_hi_s, 1)

            def root_guess(g, ln, ve_s, lnv_s, guess_s):
                if live(g):
                    wait(act, ve_s, g)
                    act.activation(ln[:, 9:10], ln[:, 8:9], ACT.Ln).then_inc(lnv_s, 1)
                    wait(act, lnv_s, g)
                    act.activation(ln[:, 10:11], ln[:, 9:10], ACT.Exp, scale=-0.5).then_inc(guess_s, 1)

            def relu_part3(g):
                if live(g):
                    wait(act, av3_s, g)
                    wait(act, x1_relu3_s, g - 1)
                    act.activation(relu3[:, :], heads[:, 0, :], ACT.Relu, scale=1.0 - SLOPE).then_inc(relu3_s, 1)

            def xl_halves(g):
                if live(g):
                    wait(act, xl_s, g)
                    wait(act, av1_s, g - 1, 2)
                    act.activation(xl_hi[:, :], xl[:, 0:HF], ACT.Copy).then_inc(xl_hi_s, 1)

            def project1(g):
                if live(g):
                    wait(act, top1_s, g)
                    wait(act, e1_s, g - 1)
                    for k in range(H):
                        last = act.activation(z1[:, k, :], score[:, k * N:(k + 1) * N], ACT.Identity,
                                              bias=att1[:, H + k:H + k + 1])
                    last.then_inc(z1_s, 1)

            def exp1(g):
                if live(g):
                    wait(act, e1_s, g)
                    wait(act, nmax1_s, g)
                    wait(act, p1_n_s, g - 1)
                    wait(act, rden1_s, g - 1)
                    for k in range(H):
                        act.activation(p1[:, k, :], e1[:, k, :], ACT.Exp, bias=nmax1[:, k:k + 1],
                                       accum_out=den1[:, k:k + 1]).then_inc(p1_s, 1)

            def p1_halves(g):
                if live(g):
                    wait(act, pt1_s, g)
                    wait(act, av1_s, g - 1, 2)
                    act.activation(p1_hi[:, :, :].rearrange("p a b -> p (a b)"), score[:, :],
                                   ACT.Copy).then_inc(p1_hi_s, 1)

            def x2_copy(g):
                if live(g):
                    wait(act, att2_s, g)
                    wait(act, x2_lo_s, g - 1)
                    wait(act, x2_hi_s, g - 1)
                    act.activation(x2[:, :].rearrange("p (a b) -> p a b", a=2), pair[:, :, 0:C2P],
                                   ACT.Copy).then_inc(x2_s, 1)

            def x2_halves(g):
                if live(g):
                    wait(act, x2_s, g)
                    wait(act, av2_s, g - 1)
                    act.activation(x2_hi[:, :], x2[:, :], ACT.Copy).then_inc(x2_hi_s, 1)

            def exp2(g):
                if live(g):
                    wait(act, e2_s, g)
                    wait(act, nmax2_s, g)
                    wait(act, pt2_s, g - 1)
                    wait(act, rden2_s, g - 1)
                    act.activation(p2[:, :], e2[:, :], ACT.Exp, bias=nmax2[:, 0:1],
                                   accum_out=den2[:, 0:1]).then_inc(p2_s, 1)

            def p2_halves(g):
                if live(g):
                    wait(act, pt2_s, g)
                    wait(act, av2_s, g - 1)
                    act.activation(p2_hi[:, :], wide[:, 2, 0:N], ACT.Copy).then_inc(p2_hi_s, 1)

            def elu_negative(g, b):
                if live(g):
                    if isinstance(g, int) and g == 0 and b == 0:
                        act.wait_ge(raw_att, TILES)
                    wait(act, av1_s, g, 2, 1 - b)
                    wait(act, ex_s, g - 1, 2)
                    cols = slice(b * 512, (b + 1) * 512)
                    act.activation(neg[:, cols], heads[:, b, :], ACT.Relu, scale=-1.0).then_inc(neg_s, 1)
                    wait(act, neg_s, g, 2, 1 - b)
                    wait(act, h_s, g - 1, 2)
                    act.activation(ex[:, cols], neg[:, cols], ACT.Exp, scale=-1.0).then_inc(ex_s, 1)

            def step(i, c):
                if isinstance(i, int) and i == 0:
                    xt_halves(0, 0)
                wh_halves(i - 3)
                xt_halves(i + 1, 1 - c)
                ht_halves(i - 1)
                root_guess(i - 2, ln2, ve2_s, lnv2_s, guess2_s)
                exp3(i - 3)
                xl_halves(i)
                project1(i)
                x1_halves(i - 2)
                relu_part3(i - 3)
                exp1(i)
                x2_copy(i - 1)
                x2_halves(i - 1)
                p1_halves(i)
                exp2(i - 1)
                p2_halves(i - 1)
                wh_copy(i - 2)
                root_guess(i - 3, ln3, ve3_s, lnv3_s, guess3_s)
                elu_negative(i, 0)
                elu_negative(i, 1)

            run(act, step)

        @block.vector
        def _(dve):
            dve.wait_ge(vectors_in, 5 * 16)
            dve.memset(b1_rows[:, HF:C1], 0.0).then_inc(raw_pads, 1)
            product = 0
            for t, (name, kt, cols, _hi, _lo, _src) in enumerate(weight_tiles()):
                raw = w_raw[:, t % 2, :]
                dve.wait_ge(raw_in[t % 2], 16 * (t // 2 + 1))
                if name == "w1":
                    vecs = [(rows[:, k * F:(k + 1) * F], k * F, F)
                            for rows in (a_src1_rows, a_dst1_rows) for k in range(H)]
                    base = HF
                else:
                    rows = a2_rows if name == "w2" else a3_rows
                    vecs = [(rows[:, j, :], 0, D) for j in range(2)]
                    base = D
                if name != "w1":
                    if t >= 2:
                        dve.wait_ge(w_hi_made, t - 1)
                        dve.wait_ge(w_lo_made, t - 1)
                    dve.memset(raw[:, base + 2:base + 4], 0.0)
                for j, (vec, at, n) in enumerate(vecs):
                    if j >= HF // n:
                        dve.wait_ge(product_used, product)
                    product += 1
                    scratch = ex[:, j * n % HF:j * n % HF + n]
                    dve.tensor_tensor_reduce(scratch, raw[:, at:at + n], vec, 1.0, 0.0, ALU.mult, ALU.add,
                                             raw[:, base + j:base + j + 1]).then_inc(product_used, 1)
                dve.wait_ge(product_used, product)
                dve.sem_inc(raw_att, 1)
                dve.wait_ge(raw_att, t + 1)
            dve.wait_ge(bias_in, 2 * 16)

            def top_of(g, dst, src, bc_s, top_s):
                if live(g):
                    wait(dve, bc_s, g)
                    dve.tensor_reduce(dst, src, AX.X, ALU.max).then_inc(top_s, 1)

            def negative_top(g, top, dst_col, ntop, top_s, ntop_s):
                if live(g):
                    wait(dve, top_s, g)
                    dve.scalar_tensor_tensor(out=ntop[:, :], in0=top[:, :], scalar=-1.0, in1=dst_col,
                                             op0=ALU.mult, op1=ALU.subtract).then_inc(ntop_s, 1)

            def negative_max(g, ntop, nmax, ntop_s, nmax_s, p_s, per):
                if live(g):
                    wait(dve, ntop_s, g)
                    wait(dve, p_s, g - 1, per)
                    dve.scalar_tensor_tensor(out=nmax[:, :], in0=ntop[:, :], scalar=SLOPE, in1=ntop[:, :],
                                             op0=ALU.mult, op1=ALU.min).then_inc(nmax_s, 1)

            def project(g, z, src, dst_col, e_s, z_s):
                if live(g):
                    wait(dve, e_s, g - 1)
                    dve.tensor_scalar(z[:, :], src, dst_col, None, ALU.add).then_inc(z_s, 1)

            def leaky(g, z, e, z_s, e_s, p_s, per):
                if live(g):
                    wait(dve, z_s, g)
                    wait(dve, p_s, g - 1, per)
                    dve.scalar_tensor_tensor(out=e, in0=z, scalar=SLOPE, in1=z,
                                             op0=ALU.mult, op1=ALU.max).then_inc(e_s, 1)

            def mask_of(dst, g, c, done):
                wait_dma(dve, adj_in, g, c)
                dve.tensor_scalar(dst, adj[:, c, :], 0.0, MASKED, ALU.is_le, ALU.mult).then_inc(done, 1)

            def make_mask1(g, c):
                if live(g):
                    wait(dve, bcast3_s, g - 2)
                    mask_of(mask1[:, c, :], g, c, mask1_s)

            def make_mask_t(g, c):
                if live(g):
                    wait(dve, mask0_s, g - 1)
                    mask_of(mask_t[:, :], g, c, mask_t_s)

            def att_wh(g):
                if live(g):
                    wait(dve, xw3_s, g)
                    dve.tensor_copy(att3[:, :], wide[:, 1, S2:S2 + 2]).then_inc(att3_s, 1)

            def elu(g, b):
                if live(g):
                    wait(dve, ex_s, g, 2, 1 - b)
                    wait(dve, ht_s, g - 1, 2)
                    cols = slice(b * 512, (b + 1) * 512)
                    dve.scalar_tensor_tensor(out=h[:, cols], in0=heads[:, b, :], scalar=0.0, in1=ex[:, cols],
                                             op0=ALU.max, op1=ALU.add).then_inc(h_s, 1)

            def residual2(g, c):
                if live(g):
                    wait(dve, av2_s, g)
                    wait(dve, x_b2_s, g)
                    dve.scalar_tensor_tensor(out=y2[:, :], in0=pair[:, 0, :], scalar=rden2[:, 0:1],
                                             in1=x_b2[:, c, :], op0=ALU.mult, op1=ALU.add).then_inc(y2_s, 1)

            def statistics(g, ln, y, y_s, bn_s):
                if live(g):
                    wait(dve, y_s, g)
                    dve.bn_stats(ln[:, 0:6], y[:, :]).then_inc(bn_s, 1)

            def mean_variance(g, ln, bn_s, mv_s):
                if live(g):
                    dve.wait_ge(bias_in, 2 * 16)
                    wait(dve, bn_s, g)
                    dve.bn_aggr(ln[:, 6:8], ln[:, 0:6]).then_inc(mv_s, 1)

            def add_eps(g, ln, mv_s, ve_s):
                if live(g):
                    wait(dve, mv_s, g)
                    dve.tensor_scalar(ln[:, 8:9], ln[:, 7:8], EPS, None, ALU.add).then_inc(ve_s, 1)

            def newton_step(g, ln, guess_s, step_s):
                if live(g):
                    wait(dve, guess_s, g)
                    dve.scalar_tensor_tensor(out=ln[:, 11:12], in0=ln[:, 10:11], scalar=ln[:, 10:11],
                                             in1=ln[:, 8:9], op0=ALU.mult, op1=ALU.mult).then_inc(step_s, 1)

            def newton_factor(g, ln, step_s, factor_s):
                if live(g):
                    wait(dve, step_s, g)
                    dve.tensor_scalar(ln[:, 12:13], ln[:, 11:12], -0.5, 1.5, ALU.mult,
                                      ALU.add).then_inc(factor_s, 1)

            def newton_root(g, ln, factor_s, rstd_s):
                if live(g):
                    wait(dve, factor_s, g)
                    dve.tensor_tensor(ln[:, 13:14], ln[:, 12:13], ln[:, 10:11], ALU.mult).then_inc(rstd_s, 1)

            def normalise2(g, c):
                if live(g):
                    wait(dve, rstd2_s, g)
                    wait(dve, x1_relu3_s, g - 2)
                    dve.tensor_scalar(x1[:, c, :], y2[:, :], ln2[:, 6:7], ln2[:, 13:14],
                                      ALU.subtract, ALU.mult).then_inc(x1_s, 1)

            def denominator(g, den, rden, p_s, per, used_s, rden_s):
                if live(g):
                    wait(dve, p_s, g, per)
                    wait(dve, used_s, g - 1)
                    dve.reciprocal(rden[:, :], den[:, :]).then_inc(rden_s, 1)

            def p3_rest(g):
                if live(g):
                    wait(dve, p3_hi_s, g)
                    wait(dve, av3_s, g - 1)
                    dve.scalar_tensor_tensor(out=p3_lo[:, :], in0=p3[:, :], scalar=rden3[:, 0:1], in1=p3_hi[:, :],
                                             op0=ALU.mult, op1=ALU.subtract).then_inc(p3_lo_s, 1)

            def x1_rest(g):
                if live(g):
                    wait(dve, x1_hi_s, g)
                    wait(dve, xw3_s, g - 1)
                    dve.tensor_tensor(x1_lo[:, :], wide[:, 2, :], x1_hi[:, :], ALU.subtract).then_inc(x1_lo_s, 1)

            def ht_rest(g, halves):
                if live(g):
                    for half in halves:
                        cols = slice(half * 512, (half + 1) * 512)
                        wait(dve, ht_hi_s, g, 2, 1 - half)
                        wait(dve, hw2_s, g - 1)
                        dve.scalar_tensor_tensor(out=ht_lo[:, cols], in0=heads[:, half, :], scalar=-1.0,
                                                 in1=ht_hi[:, cols], op0=ALU.add, op1=ALU.subtract).then_inc(ht_lo_s, 1)

            def residual3(g):
                if live(g):
                    wait(dve, x1_relu3_s, g)
                    dve.scalar_tensor_tensor(out=y3[:, :], in0=heads[:, 0, :], scalar=SLOPE, in1=x1_relu3[:, :],
                                             op0=ALU.mult, op1=ALU.add).then_inc(y3_s, 1)

            def normalise3(g, c):
                if live(g):
                    wait(dve, rstd3_s, g)
                    wait_dma(dve, res_out, g - 2, c)
                    dve.tensor_scalar(res[:, c, :], y3[:, :], ln3[:, 6:7], ln3[:, 13:14],
                                      ALU.subtract, ALU.mult).then_inc(res_s, 1)

            def att_xl(g):
                if live(g):
                    wait(dve, xw1_s, g)
                    wait(dve, bcast1_s, g - 1)
                    wait(dve, z1_s, g - 1)
                    dve.tensor_copy(att1[:, :], wide[:, 2, S1:S1 + 2 * H]).then_inc(att1_s, 1)

            def bias_xl(g):
                if live(g):
                    wait(dve, xl_hi_s, g - 1)
                    wait(dve, xl_lo_s, g - 1)
                    dve.tensor_tensor(xl[:, :].rearrange("p (a b) -> p a b", a=3), wide[:, :, 0:C1P],
                                      b1_rows[:, :].rearrange("p (a b) -> p a b", a=3),
                                      ALU.add).then_inc(xl_s, 1)

            def att_h(g):
                if live(g):
                    wait(dve, hw2_s, g)
                    dve.tensor_copy(att2[:, :], pair[:, 1, S2:S2 + 2]).then_inc(att2_s, 1)

            def p1_rest(g):
                if live(g):
                    wait(dve, p1_hi_s, g)
                    wait(dve, av1_s, g - 1, 2)
                    dve.tensor_tensor(p1_lo[:, :, :].rearrange("p a b -> p (a b)"), score[:, :],
                                      p1_hi[:, :, :].rearrange("p a b -> p (a b)"),
                                      ALU.subtract).then_inc(p1_lo_s, 1)

            def p2_rest(g):
                if live(g):
                    wait(dve, p2_hi_s, g)
                    wait(dve, av2_s, g - 1)
                    dve.tensor_tensor(p2_lo[:, :], wide[:, 2, 0:N], p2_hi[:, :], ALU.subtract).then_inc(p2_lo_s, 1)

            score_rows = score[:, :].rearrange("p (k s) -> p k s", k=H)

            def step(i, c):
                if isinstance(i, int) and i == 0:
                    make_mask_t(0, 0)
                elu(i - 1, 0)
                newton_step(i - 4, ln3, guess3_s, step3_s)
                newton_factor(i - 4, ln3, step3_s, factor3_s)
                elu(i - 1, 1)
                newton_root(i - 4, ln3, factor3_s, rstd3_s)
                residual2(i - 2, c)
                normalise3(i - 4, c)
                statistics(i - 2, ln2, y2, y2_s, bn2_s)
                top_of(i - 3, top3[:, :], pair[:, 1, 0:N], bcast3_s, top3_s)
                make_mask1(i - 1, 1 - c)
                mean_variance(i - 2, ln2, bn2_s, mv2_s)
                negative_top(i - 3, top3, att3[:, 1:2], ntop3, top3_s, ntop3_s)
                ht_rest(i - 1, [0])
                add_eps(i - 2, ln2, mv2_s, ve2_s)
                project(i - 3, z3, pair[:, 1, 0:N], att3[:, 1:2], e3_s, z3_s)
                negative_max(i - 3, ntop3, nmax3, ntop3_s, nmax3_s, p3_s, 1)
                leaky(i - 3, z3[:, :], e3[:, :], z3_s, e3_s, p3_s, 1)
                ht_rest(i - 1, [1])
                newton_step(i - 2, ln2, guess2_s, step2_s)
                att_xl(i)
                newton_factor(i - 2, ln2, step2_s, factor2_s)
                denominator(i - 3, den3, rden3, p3_s, 1, p3_lo_s, rden3_s)
                newton_root(i - 2, ln2, factor2_s, rstd2_s)
                p3_rest(i - 3)
                bias_xl(i)
                normalise2(i - 2, c)
                top_of(i, top1[:, :], score_rows, bcast1_s, top1_s)
                make_mask_t(i + 1, 1 - c)
                negative_top(i, top1, att1[:, H:2 * H], ntop1, top1_s, ntop1_s)
                negative_max(i, ntop1, nmax1, ntop1_s, nmax1_s, p1_s, H)
                leaky(i, z1[:, :, :], e1[:, :, :], z1_s, e1_s, p1_s, H)
                x1_rest(i - 2)
                denominator(i, den1, rden1, p1_s, H, p1_n_s, rden1_s)
                att_h(i - 1)
                residual3(i - 3)
                top_of(i - 1, top2[:, :], wide[:, 2, 0:N], bcast2_s, top2_s)
                project(i - 1, z2, wide[:, 2, 0:N], att2[:, 1:2], e2_s, z2_s)
                negative_top(i - 1, top2, att2[:, 1:2], ntop2, top2_s, ntop2_s)
                leaky(i - 1, z2[:, :], e2[:, :], z2_s, e2_s, p2_s, 1)
                negative_max(i - 1, ntop2, nmax2, ntop2_s, nmax2_s, p2_s, 1)
                statistics(i - 3, ln3, y3, y3_s, bn3_s)
                p1_rest(i)
                mean_variance(i - 3, ln3, bn3_s, mv3_s)
                denominator(i - 1, den2, rden2, p2_s, 1, y2_s, rden2_s)
                add_eps(i - 3, ln3, mv3_s, ve3_s)
                att_wh(i - 2)
                p2_rest(i - 1)

            run(dve, step)

        @block.gpsimd
        def _(pool):
            pool.memset(ident[:, :], 0.0).then_inc(ident_zero, 1)
            pool.wait_ge(ident_zero, 1)
            pool.affine_select(out=ident[:, :], in_=ident[:, :], compare_op=ALU.not_equal, fill=1.0, base=0,
                               pattern=[[-1, P]], channel_multiplier=1).then_inc(ident_made, 1)
            pool.wait_ge(ident_made, 1)
            pool.tensor_copy(ident_b[:, :], ident[:, :])
            pool.tensor_scalar(not_eye[:, :], ident[:, :], -1.0, 1.0, ALU.mult, ALU.add).then_inc(consts_made, 1)
            for t, (_n, kt, cols, hi, lo, _src) in enumerate(weight_tiles()):
                pool.wait_ge(w_hi_made, t + 1)
                pool.tensor_tensor(lo, w_raw[:, t % 2, 0:cols], hi, ALU.subtract).then_inc(w_lo_made, 1)
            pool.wait_ge(consts_made, 1)
            pool.wait_ge(bias_in, 2 * 16)

            def residual_bias(g, c):
                if live(g):
                    wait_dma(pool, x_in_s, g, c)
                    wait(pool, y2_s, g - 2)
                    pool.tensor_tensor(x_b2[:, c, :], x_in[:, c, :], b2_rows[:, :], ALU.add).then_inc(x_b2_s, 1)

            def residual_relu(g, c):
                if live(g):
                    wait(pool, relu3_s, g)
                    wait(pool, x1_s, g)
                    wait(pool, y3_s, g - 1)
                    pool.tensor_tensor(x1_relu3[:, :], x1[:, c, :], relu3[:, :], ALU.add).then_inc(x1_relu3_s, 1)

            def make_mask0(g, c):
                if live(g):
                    wait(pool, mask_t_s, g)
                    wait(pool, bcast2_s, g - 2)
                    pool.tensor_tensor(mask0[:, c, :], mask_t[:, :], not_eye[:, :], ALU.mult).then_inc(mask0_s, 1)

            def xl_rest(g):
                if live(g):
                    wait(pool, xl_hi_s, g)
                    wait(pool, av1_s, g - 1, 2)
                    pool.tensor_tensor(xl_lo[:, :], xl[:, 0:HF], xl_hi[:, :], ALU.subtract).then_inc(xl_lo_s, 1)

            def xt_rest(g, c):
                if live(g):
                    wait(pool, xt_hi_s, g)
                    wait(pool, xw1_s, g - 2)
                    pool.tensor_tensor(xt_lo[:, c, :], xt[:, c, :], xt_hi[:, c, :], ALU.subtract).then_inc(xt_lo_s, 1)

            def wh_rest(g):
                if live(g):
                    wait(pool, wh_hi_s, g)
                    wait(pool, av3_s, g - 1)
                    pool.tensor_tensor(wh_lo[:, :], wh[:, :], wh_hi[:, :], ALU.subtract).then_inc(wh_lo_s, 1)

            def x2_rest(g):
                if live(g):
                    wait(pool, x2_hi_s, g)
                    wait(pool, av2_s, g - 1)
                    pool.tensor_tensor(x2_lo[:, :], x2[:, :], x2_hi[:, :], ALU.subtract).then_inc(x2_lo_s, 1)

            def normalise_p1(g):
                if live(g):
                    wait(pool, rden1_s, g)
                    wait(pool, pt1_s, g - 1)
                    pool.tensor_tensor(p1_n[:, :, :], p1[:, :, :], rden1[:, :].unsqueeze(2).broadcast_to([P, H, N]),
                                       ALU.mult).then_inc(p1_n_s, 1)

            def step(i, c):
                if isinstance(i, int) and i == 0:
                    make_mask0(0, 0)
                    xt_rest(0, 0)
                wh_rest(i - 3)
                xt_rest(i + 1, 1 - c)
                residual_bias(i - 1, 1 - c)
                xl_rest(i)
                residual_relu(i - 3, 1 - c)
                normalise_p1(i)
                x2_rest(i - 1)
                make_mask0(i + 1, 1 - c)

            run(pool, step)


def kernel(x, adj, L0_gnn_W1, L0_gnn_att_src1, L0_gnn_att_dst1, L0_gnn_b1, L0_gnn_W2, L0_gnn_att_src2,
           L0_gnn_att_dst2, L0_gnn_b2, L1_gnn_W, L1_gnn_a):
    import numpy as np
    import concourse.bacc as bacc
    from concourse.bass_utils import run_bass_kernel_spmd

    x, adj = np.asarray(x), np.asarray(adj)
    B, N, D = x.shape
    given = {
        "x": x,
        "x_t": x.reshape(B, N, D // P, P).transpose(0, 3, 2, 1).reshape(B, P, D),
        "adj_t": adj.transpose(0, 2, 1),
        "w1": L0_gnn_W1, "a_src1": L0_gnn_att_src1, "a_dst1": L0_gnn_att_dst1, "b1": L0_gnn_b1,
        "w2": L0_gnn_W2, "a_src2": L0_gnn_att_src2, "a_dst2": L0_gnn_att_dst2, "b2": L0_gnn_b2,
        "w3": L1_gnn_W, "a3": L1_gnn_a,
    }
    nc = bacc.Bacc("TRN2", target_bir_lowering=False, num_devices=1)
    arrays, args = {}, {}
    for name, a in given.items():
        a = np.ascontiguousarray(a)
        arrays[f"in_{name}"] = a
        args[name] = nc.dram_tensor(f"in_{name}", a.shape, mybir.dt.from_np(a.dtype), kind="ExternalInput").ap()
    args["out"] = nc.dram_tensor("out", (B, N, D), F32, kind="ExternalOutput").ap()
    resnorm_gat_kernel(nc, **args)
    r = run_bass_kernel_spmd(nc, [arrays], core_ids=[0])
    return r.results[0]["out"]
```

```python
from contextlib import ExitStack

import concourse.bass as bass
from concourse import mybir

F32 = mybir.dt.float32
F32R = mybir.dt.float32r
BF16 = mybir.dt.bfloat16
I32 = mybir.dt.int32
ALU = mybir.AluOpType
ACT = mybir.ActivationFunctionType
AX = mybir.AxisListType

P = 128
MASKED = -9e15
SLOPE = 0.2
EPS = 1e-5


def resnorm_gat_kernel(nc, x, x_t, adj_t, w1, a_src1, a_dst1, b1, w2, a_src2, a_dst2, b2, w3, a3, out):
    B, N, D = x.shape
    H, F = a_src1.shape
    HF = H * F
    assert N == P and D % P == 0 and F == 256 and D == 512
    KT1, KT2, KT3 = D // P, HF // P, D // P
    C1 = HF + 2 * H
    C1P = C1 // 3
    C2 = D + 4
    C2P = C2 // 2
    S1 = HF - 2 * C1P
    S2 = D - C2P

    LOOP_FROM, LOOP_TO, STEPS = 6, B - 4, B + 4

    with ExitStack() as ctx:
        def sb(name, shape, dt=F32):
            return ctx.enter_context(nc.sbuf_tensor(name, shape, dt))

        def sem(name):
            return ctx.enter_context(nc.semaphore(name))

        ident = sb("ident", [P, P])
        not_eye = sb("not_eye", [P, P], BF16)
        minus_one = sb("minus_one", [P, 1])
        w1_hi, w1_lo = sb("w1_hi", [P, KT1, C1], F32R), sb("w1_lo", [P, KT1, C1], F32R)
        w2_hi, w2_lo = sb("w2_hi", [P, KT2, C2], F32R), sb("w2_lo", [P, KT2, C2], F32R)
        w3_hi, w3_lo = sb("w3_hi", [P, KT3, C2], F32R), sb("w3_lo", [P, KT3, C2], F32R)
        b1_rows = sb("b1_rows", [P, C1])
        b2_rows = sb("b2_rows", [P, D])
        w_raw = sb("w_raw", [P, 3, HF])
        wa1, wa2, wa3 = sb("wa1", [P, KT1, 2 * H]), sb("wa2", [P, KT2, 4]), sb("wa3", [P, KT3, 4])

        xt = sb("xt", [P, 2, D])
        xt_hi, xt_lo = sb("xt_hi", [P, 2, D], F32R), sb("xt_lo", [P, 2, D], F32R)
        x_in, x_b2 = sb("x_in", [P, 2, D]), sb("x_b2", [P, 2, D])
        adj = sb("adj", [P, 2, N], I32)
        mask0, mask1 = sb("mask0", [P, 2, N], BF16), sb("mask1", [P, 2, N], BF16)
        mask_t = sb("mask_t", [P, N], BF16)
        att1, att2, att3 = sb("att1", [P, 2 * H]), sb("att2", [P, 2]), sb("att3", [P, 2])
        xl = sb("xl", [P, C1])
        xl_hi, xl_lo = sb("xl_hi", [P, HF], F32R), sb("xl_lo", [P, HF], F32R)
        z1, e1, p1 = sb("z1", [P, H * N]), sb("e1", [P, H * N]), sb("p1", [P, H, N])
        p1_hi, p1_lo = sb("p1_hi", [P, H, N], F32R), sb("p1_lo", [P, H, N], F32R)
        nmax1 = sb("nmax1", [P, H])
        den1, rden1 = sb("den1", [P, H]), sb("rden1", [P, H])
        p1_n = sb("p1_n", [P, H, N])
        ex, h = sb("ex", [P, HF]), sb("h", [P, HF])
        ht_hi, ht_lo = sb("ht_hi", [P, HF], F32R), sb("ht_lo", [P, HF], F32R)
        x2 = sb("x2", [P, C2])
        x2_hi, x2_lo = sb("x2_hi", [P, C2], F32R), sb("x2_lo", [P, C2], F32R)
        z2, e2, p2 = sb("z2", [P, N]), sb("e2", [P, N]), sb("p2", [P, N])
        p2_hi, p2_lo = sb("p2_hi", [P, N], F32R), sb("p2_lo", [P, N], F32R)
        nmax2 = sb("nmax2", [P, 1])
        den2, rden2 = sb("den2", [P, 1]), sb("rden2", [P, 1])
        y2, x1 = sb("y2", [P, D]), sb("x1", [P, 2, D])
        x1_hi, x1_lo = sb("x1_hi", [P, D], F32R), sb("x1_lo", [P, D], F32R)
        wh = sb("wh", [P, C2])
        wh_hi, wh_lo = sb("wh_hi", [P, C2], F32R), sb("wh_lo", [P, C2], F32R)
        z3, e3, p3 = sb("z3", [P, N]), sb("e3", [P, N]), sb("p3", [P, N])
        p3_hi, p3_lo = sb("p3_hi", [P, N], F32R), sb("p3_lo", [P, N], F32R)
        nmax3 = sb("nmax3", [P, 1])
        den3, rden3 = sb("den3", [P, 1]), sb("rden3", [P, 1])
        relu3, x1_relu3, y3 = sb("relu3", [P, D]), sb("x1_relu3", [P, D]), sb("y3", [P, D])
        res = sb("res", [P, 2, D])
        ln2, ln3 = sb("ln2", [P, 16]), sb("ln3", [P, 16])

        wide = ctx.enter_context(nc.psum_tensor("wide", [P, 3, 512], F32))
        pair = ctx.enter_context(nc.psum_tensor("pair", [P, 2, 512], F32))
        heads = ctx.enter_context(nc.psum_tensor("heads", [P, 2, 512], F32))
        score = ctx.enter_context(nc.psum_tensor("score", [P, 512], F32))

        vectors1_in, vectors2_in, vectors3_in, bias_in = map(
            sem, ("vectors1_in", "vectors2_in", "vectors3_in", "bias_in"))
        raw_in = [sem(f"raw_in_{u}") for u in range(KT1 + KT2 // 2 + KT3 // 2)]
        xt_in, x_in_s, adj_in, res_out = (
            [sem(f"{n}_{c}") for c in range(2)] for n in ("xt_in", "x_in_s", "adj_in", "res_out"))
        ident_zero, ident_made, consts_made = sem("ident_zero"), sem("ident_made"), sem("consts_made")
        pads_made, w_hi_made, w_lo_made, product_made = map(sem, ("pads_made", "w_hi_made", "w_lo_made", "product_made"))
        wa_hi_made, wa_lo_made = sem("wa_hi_made"), sem("wa_lo_made")
        (xt_hi_s, xt_lo_s, x_b2_s, mask_t_s, mask0_s, mask1_s) = map(
            sem, ("xt_hi_s", "xt_lo_s", "x_b2_s", "mask_t_s", "mask0_s", "mask1_s"))
        (xw1_s, bcast1_s, pt1_s, av1_s, ht_s) = map(sem, ("xw1_s", "bcast1_s", "pt1_s", "av1_s", "ht_s"))
        (hw2_s, bcast2_s, pt2_s, av2_s, x1t_s) = map(sem, ("hw2_s", "bcast2_s", "pt2_s", "av2_s", "x1t_s"))
        (xw3_s, bcast3_s, av3_s) = map(sem, ("xw3_s", "bcast3_s", "av3_s"))
        (att1_s, xl_s, xl_hi_s, xl_lo_s) = map(sem, ("att1_s", "xl_s", "xl_hi_s", "xl_lo_s"))
        (nmax1_s, z1_s, e1_s, p1_s, rden1_s, p1_hi_s, p1_lo_s) = map(
            sem, ("nmax1_s", "z1_s", "e1_s", "p1_s", "rden1_s", "p1_hi_s", "p1_lo_s"))
        (p1_n_s, ex_s, h_s, ht_hi_s, ht_lo_s) = map(sem, ("p1_n_s", "ex_s", "h_s", "ht_hi_s", "ht_lo_s"))
        x2_s, wh_s = sem("x2_s"), sem("wh_s")
        (att2_s, x2_hi_s, x2_lo_s, nmax2_s, z2_s, e2_s, p2_s, rden2_s, p2_hi_s, p2_lo_s) = map(
            sem, ("att2_s", "x2_hi_s", "x2_lo_s", "nmax2_s", "z2_s", "e2_s", "p2_s",
                  "rden2_s", "p2_hi_s", "p2_lo_s"))
        (y2_s, bn2_s, mv2_s, ve2_s, lnv2_s, guess2_s, step2_s, factor2_s, rstd2_s, x1_s, x1_hi_s, x1_lo_s) = map(
            sem, ("y2_s", "bn2_s", "mv2_s", "ve2_s", "lnv2_s", "guess2_s", "step2_s", "factor2_s", "rstd2_s",
                  "x1_s", "x1_hi_s", "x1_lo_s"))
        (att3_s, wh_hi_s, wh_lo_s, nmax3_s, z3_s, e3_s, p3_s, rden3_s, p3_hi_s, p3_lo_s) = map(
            sem, ("att3_s", "wh_hi_s", "wh_lo_s", "nmax3_s", "z3_s", "e3_s", "p3_s",
                  "rden3_s", "p3_hi_s", "p3_lo_s"))
        (relu3_s, x1_relu3_s, y3_s, bn3_s, mv3_s, ve3_s, lnv3_s, guess3_s, step3_s, factor3_s, rstd3_s, res_s) = map(
            sem, ("relu3_s", "x1_relu3_s", "y3_s", "bn3_s", "mv3_s", "ve3_s", "lnv3_s", "guess3_s", "step3_s",
                  "factor3_s", "rstd3_s", "res_s"))

        def live(g):
            return not isinstance(g, int) or 0 <= g < B

        def is_step(i, n):
            return isinstance(i, int) and i == n

        def wait(eng, s, g, per=1, short=0):
            if not isinstance(g, int) or g >= 0:
                eng.wait_ge(s, g * per + (per - short))

        def wait_dma(eng, s, g, c):
            if not isinstance(g, int) or g >= 0:
                eng.wait_ge(s[c], 8 * g + (16 - 8 * c))

        def run(eng, step):
            for i in range(LOOP_FROM):
                step(i, i % 2)
            with eng.Fori(LOOP_FROM, LOOP_TO, 2) as i:
                step(i, 0)
                step(i + 1, 1)
            for i in range(LOOP_TO, STEPS):
                step(i, i % 2)

        a1_rows = (h, ex)
        a2_rows, a3_rows = res, x1
        scratch = (y3, relu3, x1_relu3)

        vectors1 = [(r[:, k * F:(k + 1) * F], k * F, F) for r in a1_rows for k in range(H)]
        vectors2 = [(a2_rows[:, j, :], 0, D) for j in range(2)]
        vectors3 = [(a3_rows[:, j, :], 0, D) for j in range(2)]
        W1, W2, W3 = ((1, HF, w1_hi, w1_lo, wa1, vectors1), (2, D, w2_hi, w2_lo, wa2, vectors2),
                      (3, D, w3_hi, w3_lo, wa3, vectors3))
        slots = [w_raw[:, 0], w_raw[:, 1], w_raw[:, 2], xl[:, 0:HF]] + [w_raw[:, u % 3] for u in range(6)]
        parts = []
        for w, src, kts, per in ((W1, w1, KT1, 1), (W2, w2, KT2, 2), (W3, w3, KT3, 2)):
            for kt in range(0, kts, per):
                u = len(parts)
                done = parts[-1][6] + parts[-1][2] * len(parts[-1][0][5]) if parts else 0
                parts.append((w, kt, per, src, slots[u].rearrange("p (t n) -> p t n", t=per),
                              u - (4 if u < 7 else 3), done))
        PARTS1, PARTS2, PARTS3 = range(4), range(4, 8), range(8, 10)

        def products_through(u):
            return parts[u][6] + parts[u][2] * len(parts[u][0][5])

        def wait_weight(eng, us):
            eng.wait_ge(w_hi_made, us[-1] + 1)
            eng.wait_ge(w_lo_made, us[-1] + 1)
            eng.wait_ge(wa_hi_made, parts[us[0]][0][0])
            eng.wait_ge(wa_lo_made, parts[us[0]][0][0])

        block = ctx.enter_context(nc.Block())

        @block.sync
        def _(sp):
            def rows(v, n):
                return v.unsqueeze(0).broadcast_to([P, n])

            def load_part(u):
                _w, kt, n, src, raw, before, _ = parts[u]
                if before >= 0:
                    sp.wait_ge(w_hi_made, before + 1)
                    sp.wait_ge(w_lo_made, before + 1)
                    sp.wait_ge(product_made, products_through(before))
                sp.dma_start(raw, src[kt * P:(kt + n) * P, :].rearrange("(t p) n -> p t n", p=P)).then_inc(raw_in[u], 16)

            def load_xt(g, c):
                if live(g):
                    wait(sp, xt_hi_s, g - 2)
                    wait(sp, xt_lo_s, g - 2)
                    sp.dma_start(xt[:, c, :], x_t[g]).then_inc(xt_in[c], 16)

            def load_x(g, c):
                if live(g):
                    wait(sp, x_b2_s, g - 2)
                    sp.dma_start(x_in[:, c, :], x[g]).then_inc(x_in_s[c], 16)

            def load_adj(g, c):
                if live(g):
                    wait(sp, mask_t_s, g - 2)
                    wait(sp, mask1_s, g - 2)
                    sp.dma_start(adj[:, c, :], adj_t[g]).then_inc(adj_in[c], 16)

            def step(i, c):
                load_x(i, c)
                load_xt(i + 2, c)
                load_adj(i + 1, 1 - c)
                if is_step(i, 0):
                    load_part(PARTS3[1])
                g = i - 4
                if live(g):
                    wait(sp, res_s, g)
                    sp.dma_start(out[g], res[:, c, :]).then_inc(res_out[c], 16)

            load_xt(0, 0)
            load_part(0)
            sp.dma_start(a1_rows[0][:, :], rows(a_src1.rearrange("h f -> (h f)"), HF)).then_inc(vectors1_in, 16)
            sp.dma_start(a1_rows[1][:, :], rows(a_dst1.rearrange("h f -> (h f)"), HF)).then_inc(vectors1_in, 16)
            for u in PARTS1[1:]:
                load_part(u)
            sp.dma_start(a2_rows[:, 0, :], rows(a_src2.rearrange("h f -> (h f)"), D)).then_inc(vectors2_in, 16)
            sp.dma_start(a2_rows[:, 1, :], rows(a_dst2.rearrange("h f -> (h f)"), D)).then_inc(vectors2_in, 16)
            sp.dma_start(b1_rows[:, 0:HF], rows(b1, HF)).then_inc(bias_in, 16)
            sp.dma_start(b2_rows[:, :], rows(b2, D)).then_inc(bias_in, 16)
            load_adj(0, 0)
            load_xt(1, 1)
            sp.dma_start(a3_rows[:, :, :].rearrange("p a b -> p (a b)"),
                         rows(a3.rearrange("f o -> (f o)"), 2 * D)).then_inc(vectors3_in, 16)
            for u in (*PARTS2, PARTS3[0]):
                load_part(u)
            run(sp, step)
            for c in range(2):
                sp.wait_ge(res_out[c], 16 * (B // 2))

        @block.tensor
        def _(pe):
            pe.wait_ge(consts_made, 1)

            def split_matmul(dst, k, kts, lhs, rhs, last=None):
                n = 0
                for a, b in ((0, 0), (0, 1), (1, 0)):
                    for ch, d in enumerate(dst):
                        mm = pe.matmul(d, lhs[a], rhs[b](ch), start=(k == 0 and n == 0),
                                       stop=(k == kts - 1 and n == 2), skip_group_check=True)
                    n += 1
                return mm

            def xw1(g, c, kts):
                if not live(g):
                    return
                if kts[0] == 0:
                    if isinstance(g, int) and g == 0:
                        wait_weight(pe, PARTS1)
                    wait(pe, xt_hi_s, g)
                    wait(pe, xt_lo_s, g)
                    wait(pe, wh_s, g - 3)
                    wait(pe, p2_lo_s, g - 2)
                for k in kts:
                    mm = split_matmul(
                        [wide[:, ch, 0:C1P] for ch in range(3)], k, KT1,
                        (xt_hi[:, c, k * P:(k + 1) * P], xt_lo[:, c, k * P:(k + 1) * P]),
                        (lambda ch: w1_hi[:, k, ch * C1P:(ch + 1) * C1P],
                         lambda ch: w1_lo[:, k, ch * C1P:(ch + 1) * C1P]))
                if kts[-1] == KT1 - 1:
                    mm.then_inc(xw1_s, 1)

            def hw2(g, kts):
                if not live(g):
                    return
                if kts[0] == 0:
                    if isinstance(g, int) and g == 0:
                        wait_weight(pe, PARTS2)
                    wait(pe, y2_s, g - 1)
                    wait(pe, z3_s, g - 2)
                for k in kts:
                    if k in (0, KT2 // 2):
                        half = 1 if k == 0 else 0
                        wait(pe, ht_hi_s, g, 2, half)
                        wait(pe, ht_lo_s, g, 2, half)
                    mm = split_matmul(
                        [pair[:, ch, 0:C2P] for ch in range(2)], k, KT2,
                        (ht_hi[:, k * P:(k + 1) * P], ht_lo[:, k * P:(k + 1) * P]),
                        (lambda ch: w2_hi[:, k, ch * C2P:(ch + 1) * C2P],
                         lambda ch: w2_lo[:, k, ch * C2P:(ch + 1) * C2P]))
                if kts[-1] == KT2 - 1:
                    mm.then_inc(hw2_s, 1)

            def xw3(g, kts):
                if not live(g):
                    return
                if kts[0] == 0:
                    if isinstance(g, int) and g == 0:
                        wait_weight(pe, PARTS3)
                    wait(pe, x1_hi_s, g)
                    wait(pe, x1_lo_s, g)
                    if not isinstance(g, int) or g + 2 < B:
                        wait(pe, xl_s, g + 2)
                for k in kts:
                    mm = split_matmul(
                        [wide[:, ch, 0:C2P] for ch in range(2)], k, KT3,
                        (x1_hi[:, k * P:(k + 1) * P], x1_lo[:, k * P:(k + 1) * P]),
                        (lambda ch: w3_hi[:, k, ch * C2P:(ch + 1) * C2P],
                         lambda ch: w3_lo[:, k, ch * C2P:(ch + 1) * C2P]))
                if kts[-1] == KT3 - 1:
                    mm.then_inc(xw3_s, 1)

            def spread(dst, col, n, done):
                for k in range(n):
                    mm = pe.matmul(dst[:, k * N:(k + 1) * N], col[:, k:k + 1].broadcast_to([P, P]), ident[:, :],
                                   is_transpose=True, start=(k == 0), stop=(k == n - 1), skip_group_check=True)
                mm.then_inc(done, 1)

            def bcast1(g):
                if live(g):
                    wait(pe, att1_s, g)
                    wait(pe, p1_lo_s, g - 1)
                    spread(score, att1, H, bcast1_s)

            def bcast2(g):
                if live(g):
                    wait(pe, att2_s, g)
                    wait(pe, x1_lo_s, g - 1)
                    spread(wide[:, 2, :], att2, 1, bcast2_s)

            def bcast3(g):
                if live(g):
                    wait(pe, att3_s, g)
                    spread(pair[:, 1, :], att3, 1, bcast3_s)

            def pt1(g):
                if live(g):
                    wait(pe, p1_n_s, g)
                    for k in range(H):
                        mm = pe.transpose(score[:, k * N:(k + 1) * N], p1_n[:, k, :], ident[:, :])
                    mm.then_inc(pt1_s, 1)

            def pt2(g):
                if live(g):
                    wait(pe, p2_s, g)
                    pe.transpose(wide[:, 2, 0:N], p2[:, :], ident[:, :]).then_inc(pt2_s, 1)

            def av1(g):
                if live(g):
                    wait(pe, p1_hi_s, g)
                    wait(pe, xl_hi_s, g)
                    wait(pe, xl_lo_s, g)
                    wait(pe, y3_s, g - 3)
                    for k in range(H):
                        for n, v in enumerate((xl_hi, xl_lo)):
                            pe.matmul(heads[:, k // 2, (k % 2) * F:(k % 2 + 1) * F], p1_hi[:, k, :],
                                      v[:, k * F:(k + 1) * F], start=(k % 2 == 0 and n == 0), stop=False,
                                      skip_group_check=True)
                    wait(pe, p1_lo_s, g)
                    for k in range(H):
                        mm = pe.matmul(heads[:, k // 2, (k % 2) * F:(k % 2 + 1) * F], p1_lo[:, k, :],
                                       xl_hi[:, k * F:(k + 1) * F], start=False, stop=(k % 2 == 1),
                                       skip_group_check=True)
                        if k % 2 == 1:
                            mm.then_inc(av1_s, 1)

            def ht(g):
                if live(g):
                    for half in range(2):
                        wait(pe, h_s, g, 2, 0)
                        for k in range(4):
                            f = half * 4 + k
                            mm = pe.transpose(heads[:, half, k * P:(k + 1) * P], h[:, f * P:(f + 1) * P],
                                              ident[:, :])
                        mm.then_inc(ht_s, 1)

            def av_wide(dst, p_hi, p_lo, v_hi, v_lo, done):
                for n, (a, b) in enumerate(((p_hi, v_hi), (p_hi, v_lo), (p_lo, v_hi))):
                    mm = pe.matmul(dst, a[:, :], b[:, 0:D], start=(n == 0), stop=(n == 2))
                mm.then_inc(done, 1)

            def av2(g):
                if live(g):
                    wait(pe, p2_hi_s, g)
                    wait(pe, p2_lo_s, g)
                    wait(pe, x2_hi_s, g)
                    wait(pe, x2_lo_s, g)
                    av_wide(pair[:, 0, :], p2_hi, p2_lo, x2_hi, x2_lo, av2_s)

            def x1t(g, c):
                if live(g):
                    wait(pe, x1_s, g)
                    if not isinstance(g, int) or g + 2 < B:
                        wait(pe, xl_s, g + 2)
                    for k in range(KT3):
                        mm = pe.transpose(wide[:, 2, k * P:(k + 1) * P], x1[:, c, k * P:(k + 1) * P],
                                          ident[:, :])
                    mm.then_inc(x1t_s, 1)

            def av3(g):
                if live(g):
                    wait(pe, p3_hi_s, g)
                    wait(pe, p3_lo_s, g)
                    wait(pe, wh_hi_s, g)
                    wait(pe, wh_lo_s, g)
                    if not isinstance(g, int) or g + 2 < B:
                        wait(pe, ht_lo_s, g + 2, 2)
                    av_wide(heads[:, 0, :], p3_hi, p3_lo, wh_hi, wh_lo, av3_s)

            def step(i, c):
                xw1(i, c, [0])
                bcast3(i - 3)
                xw1(i, c, [1])
                ht(i - 1)
                xw1(i, c, [2, 3])
                hw2(i - 1, [0])
                bcast1(i)
                hw2(i - 1, [1, 2, 3, 4])
                x1t(i - 2, c)
                hw2(i - 1, [5])
                av3(i - 3)
                hw2(i - 1, [6, 7])
                xw3(i - 2, [0])
                bcast2(i - 1)
                xw3(i - 2, [1])
                pt1(i)
                xw3(i - 2, [2, 3])
                pt2(i - 1)
                av1(i)
                av2(i - 1)

            run(pe, step)

        @block.scalar
        def _(act):
            act.preload_act_table_set("natural_log_exp_and_others")

            def weight_hi(us):
                for u in us:
                    (_, cols, hi, *_), kt, n, _src, raw, _before, _done = parts[u]
                    act.wait_ge(raw_in[u], 16)
                    act.activation(hi[:, kt:kt + n, 0:cols], raw, ACT.Copy).then_inc(w_hi_made, 1)

            def attention_hi(us):
                _, cols, hi, _lo, wa, _vectors = parts[us[0]][0]
                act.wait_ge(product_made, products_through(us[-1]))
                act.wait_ge(pads_made, 3)
                act.activation(hi[:, :, cols:], wa[:, :, :], ACT.Copy).then_inc(wa_hi_made, 1)

            def wh_copy(g):
                if live(g):
                    wait(act, att3_s, g)
                    wait(act, wh_lo_s, g - 1)
                    wait(act, wh_hi_s, g - 1)
                    act.activation(wh[:, :].rearrange("p (a b) -> p a b", a=2), wide[:, 0:2, 0:C2P],
                                   ACT.Copy).then_inc(wh_s, 1)

            def wh_halves(g):
                if live(g):
                    wait(act, wh_s, g)
                    wait(act, av3_s, g - 1)
                    act.activation(wh_hi[:, :], wh[:, :], ACT.Copy).then_inc(wh_hi_s, 1)

            def exp3(g):
                if live(g):
                    wait(act, e3_s, g)
                    wait(act, nmax3_s, g)
                    wait(act, p3_lo_s, g - 1)
                    wait(act, rden3_s, g - 1)
                    act.activation(p3[:, :], e3[:, :], ACT.Exp, bias=nmax3[:, 0:1],
                                   accum_out=den3[:, 0:1]).then_inc(p3_s, 1)
                    wait(act, rden3_s, g)
                    wait(act, av3_s, g - 1)
                    act.activation(p3_hi[:, :], p3[:, :], ACT.Copy, scale=rden3[:, 0:1]).then_inc(p3_hi_s, 1)

            def x1_halves(g):
                if live(g):
                    wait(act, x1t_s, g)
                    wait(act, xw3_s, g - 1)
                    act.activation(x1_hi[:, :], wide[:, 2, :], ACT.Copy).then_inc(x1_hi_s, 1)

            def ht_halves(g):
                if live(g):
                    for half in range(2):
                        wait(act, ht_s, g, 2, 1 - half)
                        wait(act, hw2_s, g - 1)
                        act.activation(ht_hi[:, half * 512:(half + 1) * 512], heads[:, half, :],
                                       ACT.Copy, bias=-1.0).then_inc(ht_hi_s, 1)

            def xt_halves(g, c):
                if live(g):
                    wait_dma(act, xt_in, g, c)
                    wait(act, xw1_s, g - 2)
                    act.activation(xt_hi[:, c, :], xt[:, c, :], ACT.Copy).then_inc(xt_hi_s, 1)

            def root_guess(g, ln, ve_s, lnv_s, guess_s):
                if live(g):
                    wait(act, ve_s, g)
                    act.activation(ln[:, 9:10], ln[:, 8:9], ACT.Ln).then_inc(lnv_s, 1)
                    wait(act, lnv_s, g)
                    act.activation(ln[:, 10:11], ln[:, 9:10], ACT.Exp, scale=-0.5).then_inc(guess_s, 1)

            def relu_part3(g):
                if live(g):
                    wait(act, av3_s, g)
                    wait(act, x1_relu3_s, g - 1)
                    act.activation(relu3[:, :], heads[:, 0, :], ACT.Relu, scale=1.0 - SLOPE).then_inc(relu3_s, 1)

            def xl_halves(g):
                if live(g):
                    wait(act, xl_s, g)
                    wait(act, av1_s, g - 1, 2)
                    act.activation(xl_hi[:, :], xl[:, 0:HF], ACT.Copy).then_inc(xl_hi_s, 1)

            def exp1(g):
                if live(g):
                    wait(act, e1_s, g)
                    wait(act, nmax1_s, g)
                    wait(act, p1_n_s, g - 1)
                    wait(act, rden1_s, g - 1)
                    for k in range(H):
                        act.activation(p1[:, k, :], e1[:, k * N:(k + 1) * N], ACT.Exp, bias=nmax1[:, k:k + 1],
                                       accum_out=den1[:, k:k + 1]).then_inc(p1_s, 1)

            def p1_halves(g):
                if live(g):
                    wait(act, pt1_s, g)
                    wait(act, av1_s, g - 1, 2)
                    act.activation(p1_hi[:, :, :].rearrange("p a b -> p (a b)"), score[:, :],
                                   ACT.Copy).then_inc(p1_hi_s, 1)

            def x2_copy(g):
                if live(g):
                    wait(act, att2_s, g)
                    wait(act, x2_lo_s, g - 1)
                    wait(act, x2_hi_s, g - 1)
                    act.activation(x2[:, :].rearrange("p (a b) -> p a b", a=2), pair[:, :, 0:C2P],
                                   ACT.Copy).then_inc(x2_s, 1)

            def x2_halves(g):
                if live(g):
                    wait(act, x2_s, g)
                    wait(act, av2_s, g - 1)
                    act.activation(x2_hi[:, :], x2[:, :], ACT.Copy).then_inc(x2_hi_s, 1)

            def exp2(g):
                if live(g):
                    wait(act, e2_s, g)
                    wait(act, nmax2_s, g)
                    wait(act, pt2_s, g - 1)
                    wait(act, rden2_s, g - 1)
                    act.activation(p2[:, :], e2[:, :], ACT.Exp, bias=nmax2[:, 0:1],
                                   accum_out=den2[:, 0:1]).then_inc(p2_s, 1)

            def p2_halves(g):
                if live(g):
                    wait(act, pt2_s, g)
                    wait(act, av2_s, g - 1)
                    act.activation(p2_hi[:, :], wide[:, 2, 0:N], ACT.Copy).then_inc(p2_hi_s, 1)

            def elu_exp(g, b):
                if live(g):
                    wait(act, av1_s, g, 2, 1 - b)
                    wait(act, h_s, g - 1, 2)
                    act.activation(ex[:, b * 512:(b + 1) * 512], heads[:, b, :], ACT.Exp,
                                   bias=minus_one[:, 0:1]).then_inc(ex_s, 1)

            def step(i, c):
                wh_halves(i - 3)
                xt_halves(i + 1, 1 - c)
                root_guess(i - 2, ln2, ve2_s, lnv2_s, guess2_s)
                ht_halves(i - 1)
                exp3(i - 3)
                xl_halves(i)
                x1_halves(i - 2)
                exp1(i)
                relu_part3(i - 3)
                if is_step(i, 0):
                    attention_hi(PARTS2)
                x2_copy(i - 1)
                x2_halves(i - 1)
                p1_halves(i)
                exp2(i - 1)
                p2_halves(i - 1)
                wh_copy(i - 2)
                elu_exp(i, 0)
                elu_exp(i, 1)
                root_guess(i - 3, ln3, ve3_s, lnv3_s, guess3_s)
                if is_step(i, 0):
                    weight_hi(PARTS3[1:])
                if is_step(i, 1):
                    attention_hi(PARTS3)

            xt_halves(0, 0)
            weight_hi(PARTS1)
            attention_hi(PARTS1)
            weight_hi(PARTS2)
            weight_hi(PARTS3[:1])
            run(act, step)

        @block.vector
        def _(dve):
            def attention_columns(us, vectors_in):
                dve.wait_ge(vectors_in, 16 if vectors_in is vectors3_in else 2 * 16)
                for u in us:
                    (_, _cols, _hi, _lo, wa, vectors), kt, n, _src, raw, _before, q = parts[u]
                    dve.wait_ge(raw_in[u], 16)
                    for t in range(n):
                        for j, (vec, at, length) in enumerate(vectors):
                            if q >= len(scratch):
                                dve.wait_ge(product_made, q - len(scratch) + 1)
                            dve.tensor_tensor_reduce(scratch[q % len(scratch)][:, 0:length],
                                                     raw[:, t, at:at + length], vec, 1.0, 0.0, ALU.mult,
                                                     ALU.add, wa[:, kt + t, j:j + 1]).then_inc(product_made, 1)
                            q += 1

            def masked_scores(g, z, src, att, mask, mask_s, bc_s, e_s, z_s, heads_of=1):
                if live(g):
                    wait(dve, bc_s, g)
                    wait(dve, mask_s, g)
                    wait(dve, e_s, g - 1)
                    for k in range(heads_of):
                        last = dve.scalar_tensor_tensor(
                            out=z[:, k * N:(k + 1) * N], in0=src[:, k * N:(k + 1) * N],
                            scalar=att[:, heads_of + k:heads_of + k + 1], in1=mask, op0=ALU.add, op1=ALU.add)
                    last.then_inc(z_s, 1)

            def negative_max(g, e, nmax, e_s, nmax_s, p_s, per):
                if live(g):
                    wait(dve, e_s, g)
                    wait(dve, p_s, g - 1, per)
                    dve.tensor_reduce(nmax, e, AX.X, ALU.max, negate=True).then_inc(nmax_s, 1)

            def leaky(g, z, e, z_s, e_s, p_s, per):
                if live(g):
                    wait(dve, z_s, g)
                    wait(dve, p_s, g - 1, per)
                    dve.scalar_tensor_tensor(out=e, in0=z, scalar=SLOPE, in1=z,
                                             op0=ALU.mult, op1=ALU.max).then_inc(e_s, 1)

            def mask_of(dst, g, c, done):
                wait_dma(dve, adj_in, g, c)
                dve.tensor_scalar(dst, adj[:, c, :], 0.0, MASKED, ALU.is_le, ALU.mult).then_inc(done, 1)

            def make_mask1(g, c):
                if live(g):
                    wait(dve, z3_s, g - 2)
                    mask_of(mask1[:, c, :], g, c, mask1_s)

            def make_mask_t(g, c):
                if live(g):
                    wait(dve, mask0_s, g - 1)
                    mask_of(mask_t[:, :], g, c, mask_t_s)

            def att_wh(g):
                if live(g):
                    wait(dve, xw3_s, g)
                    dve.tensor_copy(att3[:, :], wide[:, 1, S2:S2 + 2]).then_inc(att3_s, 1)

            def elu(g, b):
                if live(g):
                    wait(dve, ex_s, g, 2, 1 - b)
                    wait(dve, ht_s, g - 1, 2)
                    cols = slice(b * 512, (b + 1) * 512)
                    dve.scalar_tensor_tensor(out=h[:, cols], in0=ex[:, cols], scalar=1.0, in1=heads[:, b, :],
                                             op0=ALU.min, op1=ALU.max).then_inc(h_s, 1)

            def residual2(g, c):
                if live(g):
                    wait(dve, av2_s, g)
                    wait(dve, x_b2_s, g)
                    wait(dve, rden2_s, g)
                    dve.scalar_tensor_tensor(out=y2[:, :], in0=pair[:, 0, :], scalar=rden2[:, 0:1],
                                             in1=x_b2[:, c, :], op0=ALU.mult, op1=ALU.add).then_inc(y2_s, 1)

            def statistics(g, ln, y, y_s, bn_s):
                if live(g):
                    wait(dve, y_s, g)
                    dve.bn_stats(ln[:, 0:6], y[:, :]).then_inc(bn_s, 1)

            def mean_variance(g, ln, bn_s, mv_s):
                if live(g):
                    dve.wait_ge(bias_in, 2 * 16)
                    wait(dve, bn_s, g)
                    dve.bn_aggr(ln[:, 6:8], ln[:, 0:6]).then_inc(mv_s, 1)

            def add_eps(g, ln, mv_s, ve_s):
                if live(g):
                    wait(dve, mv_s, g)
                    dve.tensor_scalar(ln[:, 8:9], ln[:, 7:8], EPS, None, ALU.add).then_inc(ve_s, 1)

            def newton_step(g, ln, guess_s, step_s):
                if live(g):
                    wait(dve, guess_s, g)
                    dve.scalar_tensor_tensor(out=ln[:, 11:12], in0=ln[:, 10:11], scalar=ln[:, 10:11],
                                             in1=ln[:, 8:9], op0=ALU.mult, op1=ALU.mult).then_inc(step_s, 1)

            def newton_factor(g, ln, step_s, factor_s):
                if live(g):
                    wait(dve, step_s, g)
                    dve.tensor_scalar(ln[:, 12:13], ln[:, 11:12], -0.5, 1.5, ALU.mult,
                                      ALU.add).then_inc(factor_s, 1)

            def newton_root(g, ln, factor_s, rstd_s):
                if live(g):
                    wait(dve, factor_s, g)
                    dve.tensor_tensor(ln[:, 13:14], ln[:, 12:13], ln[:, 10:11], ALU.mult).then_inc(rstd_s, 1)

            def normalise2(g, c):
                if live(g):
                    wait(dve, rstd2_s, g)
                    wait(dve, x1_relu3_s, g - 2)
                    dve.tensor_scalar(x1[:, c, :], y2[:, :], ln2[:, 6:7], ln2[:, 13:14],
                                      ALU.subtract, ALU.mult).then_inc(x1_s, 1)

            def denominator(g, den, rden, p_s, per, used_s, rden_s):
                if live(g):
                    wait(dve, p_s, g, per)
                    wait(dve, used_s, g - 1)
                    dve.reciprocal(rden[:, :], den[:, :]).then_inc(rden_s, 1)

            def p3_rest(g):
                if live(g):
                    wait(dve, p3_hi_s, g)
                    wait(dve, av3_s, g - 1)
                    dve.scalar_tensor_tensor(out=p3_lo[:, :], in0=p3[:, :], scalar=rden3[:, 0:1], in1=p3_hi[:, :],
                                             op0=ALU.mult, op1=ALU.subtract).then_inc(p3_lo_s, 1)

            def x1_rest(g):
                if live(g):
                    wait(dve, x1_hi_s, g)
                    wait(dve, xw3_s, g - 1)
                    dve.tensor_tensor(x1_lo[:, :], wide[:, 2, :], x1_hi[:, :], ALU.subtract).then_inc(x1_lo_s, 1)

            def ht_rest(g, halves):
                if live(g):
                    for half in halves:
                        cols = slice(half * 512, (half + 1) * 512)
                        wait(dve, ht_hi_s, g, 2, 1 - half)
                        wait(dve, hw2_s, g - 1)
                        dve.scalar_tensor_tensor(out=ht_lo[:, cols], in0=heads[:, half, :], scalar=-1.0,
                                                 in1=ht_hi[:, cols], op0=ALU.add, op1=ALU.subtract).then_inc(ht_lo_s, 1)

            def residual3(g):
                if live(g):
                    wait(dve, x1_relu3_s, g)
                    dve.scalar_tensor_tensor(out=y3[:, :], in0=heads[:, 0, :], scalar=SLOPE, in1=x1_relu3[:, :],
                                             op0=ALU.mult, op1=ALU.add).then_inc(y3_s, 1)

            def normalise3(g, c):
                if live(g):
                    wait(dve, rstd3_s, g)
                    wait_dma(dve, res_out, g - 2, c)
                    dve.tensor_scalar(res[:, c, :], y3[:, :], ln3[:, 6:7], ln3[:, 13:14],
                                      ALU.subtract, ALU.mult).then_inc(res_s, 1)

            def att_xl(g):
                if live(g):
                    wait(dve, xw1_s, g)
                    wait(dve, bcast1_s, g - 1)
                    wait(dve, z1_s, g - 1)
                    dve.tensor_copy(att1[:, :], wide[:, 2, S1:S1 + 2 * H]).then_inc(att1_s, 1)

            def bias_xl(g):
                if live(g):
                    wait(dve, xl_hi_s, g - 1)
                    wait(dve, xl_lo_s, g - 1)
                    dve.tensor_tensor(xl[:, :].rearrange("p (a b) -> p a b", a=3), wide[:, :, 0:C1P],
                                      b1_rows[:, :].rearrange("p (a b) -> p a b", a=3),
                                      ALU.add).then_inc(xl_s, 1)

            def att_h(g):
                if live(g):
                    wait(dve, hw2_s, g)
                    dve.tensor_copy(att2[:, :], pair[:, 1, S2:S2 + 2]).then_inc(att2_s, 1)

            def p1_rest(g):
                if live(g):
                    wait(dve, p1_hi_s, g)
                    wait(dve, av1_s, g - 1, 2)
                    dve.tensor_tensor(p1_lo[:, :, :].rearrange("p a b -> p (a b)"), score[:, :],
                                      p1_hi[:, :, :].rearrange("p a b -> p (a b)"),
                                      ALU.subtract).then_inc(p1_lo_s, 1)

            def p2_rest(g):
                if live(g):
                    wait(dve, p2_hi_s, g)
                    wait(dve, av2_s, g - 1)
                    dve.tensor_tensor(p2_lo[:, :], wide[:, 2, 0:N], p2_hi[:, :], ALU.subtract).then_inc(p2_lo_s, 1)

            def step(i, c):
                residual2(i - 2, c)
                elu(i - 1, 0)
                elu(i - 1, 1)
                statistics(i - 2, ln2, y2, y2_s, bn2_s)
                newton_step(i - 4, ln3, guess3_s, step3_s)
                mean_variance(i - 2, ln2, bn2_s, mv2_s)
                newton_factor(i - 4, ln3, step3_s, factor3_s)
                add_eps(i - 2, ln2, mv2_s, ve2_s)
                masked_scores(i - 3, z3, pair[:, 1, 0:N], att3, mask1[:, 1 - c, :], mask1_s, bcast3_s, e3_s, z3_s)
                newton_root(i - 4, ln3, factor3_s, rstd3_s)
                make_mask1(i - 1, 1 - c)
                leaky(i - 3, z3[:, :], e3[:, :], z3_s, e3_s, p3_s, 1)
                normalise3(i - 4, c)
                negative_max(i - 3, e3[:, :], nmax3[:, :], e3_s, nmax3_s, p3_s, 1)
                newton_step(i - 2, ln2, guess2_s, step2_s)
                ht_rest(i - 1, [0])
                newton_factor(i - 2, ln2, step2_s, factor2_s)
                ht_rest(i - 1, [1])
                newton_root(i - 2, ln2, factor2_s, rstd2_s)
                denominator(i - 3, den3, rden3, p3_s, 1, p3_lo_s, rden3_s)
                att_xl(i)
                bias_xl(i)
                masked_scores(i, z1, score, att1, mask0[:, c, :], mask0_s, bcast1_s, e1_s, z1_s, H)
                p3_rest(i - 3)
                normalise2(i - 2, c)
                leaky(i, z1[:, :], e1[:, :], z1_s, e1_s, p1_s, H)
                negative_max(i, e1[:, :].rearrange("p (k s) -> p k s", k=H), nmax1[:, :], e1_s, nmax1_s, p1_s, H)
                make_mask_t(i + 1, 1 - c)
                if is_step(i, 1):
                    attention_columns(PARTS3[1:], vectors3_in)
                if is_step(i, 0):
                    attention_columns(PARTS2[3:], vectors2_in)
                x1_rest(i - 2)
                denominator(i, den1, rden1, p1_s, H, p1_n_s, rden1_s)
                att_h(i - 1)
                masked_scores(i - 1, z2, wide[:, 2, 0:N], att2, mask0[:, 1 - c, :], mask0_s, bcast2_s, e2_s, z2_s)
                leaky(i - 1, z2[:, :], e2[:, :], z2_s, e2_s, p2_s, 1)
                negative_max(i - 1, e2[:, :], nmax2[:, :], e2_s, nmax2_s, p2_s, 1)
                residual3(i - 3)
                p1_rest(i)
                att_wh(i - 2)
                p2_rest(i - 1)
                denominator(i - 1, den2, rden2, p2_s, 1, y2_s, rden2_s)
                statistics(i - 3, ln3, y3, y3_s, bn3_s)
                mean_variance(i - 3, ln3, bn3_s, mv3_s)
                add_eps(i - 3, ln3, mv3_s, ve3_s)
                if is_step(i, 0):
                    attention_columns(PARTS3[:1], vectors3_in)

            dve.memset(b1_rows[:, HF:C1], 0.0).then_inc(pads_made, 1)
            dve.memset(wa2[:, :, 2:4], 0.0).then_inc(pads_made, 1)
            dve.memset(wa3[:, :, 2:4], 0.0).then_inc(pads_made, 1)
            attention_columns(PARTS1, vectors1_in)
            make_mask_t(0, 0)
            attention_columns(PARTS2[:3], vectors2_in)
            dve.wait_ge(bias_in, 2 * 16)
            dve.tensor_scalar(b1_rows[:, 0:HF], b1_rows[:, 0:HF], 1.0, None, ALU.add).then_inc(pads_made, 1)
            dve.wait_ge(pads_made, 4)
            run(dve, step)

        @block.gpsimd
        def _(pool):
            pool.memset(ident[:, :], 0.0).then_inc(ident_zero, 1)
            pool.memset(minus_one[:, :], -1.0)
            pool.wait_ge(ident_zero, 1)
            pool.affine_select(out=ident[:, :], in_=ident[:, :], compare_op=ALU.not_equal, fill=1.0, base=0,
                               pattern=[[-1, P]], channel_multiplier=1).then_inc(ident_made, 1)
            pool.wait_ge(ident_made, 1)
            pool.tensor_scalar(not_eye[:, :], ident[:, :], -1.0, 1.0, ALU.mult, ALU.add).then_inc(consts_made, 1)

            def weight_lo(us):
                for u in us:
                    (_, cols, hi, lo, *_), kt, n, _src, raw, _before, _done = parts[u]
                    pool.wait_ge(w_hi_made, u + 1)
                    pool.tensor_tensor(lo[:, kt:kt + n, 0:cols], raw, hi[:, kt:kt + n, 0:cols],
                                       ALU.subtract).then_inc(w_lo_made, 1)

            def attention_lo(us):
                number, cols, hi, lo, wa, _vectors = parts[us[0]][0]
                pool.wait_ge(wa_hi_made, number)
                pool.tensor_tensor(lo[:, :, cols:], wa[:, :, :], hi[:, :, cols:], ALU.subtract).then_inc(wa_lo_made, 1)

            def residual_bias(g, c):
                if live(g):
                    wait_dma(pool, x_in_s, g, c)
                    wait(pool, y2_s, g - 2)
                    pool.tensor_tensor(x_b2[:, c, :], x_in[:, c, :], b2_rows[:, :], ALU.add).then_inc(x_b2_s, 1)

            def residual_relu(g, c):
                if live(g):
                    wait(pool, relu3_s, g)
                    wait(pool, x1_s, g)
                    wait(pool, y3_s, g - 1)
                    pool.tensor_tensor(x1_relu3[:, :], x1[:, c, :], relu3[:, :], ALU.add).then_inc(x1_relu3_s, 1)

            def make_mask0(g, c):
                if live(g):
                    wait(pool, mask_t_s, g)
                    wait(pool, z2_s, g - 2)
                    pool.tensor_tensor(mask0[:, c, :], mask_t[:, :], not_eye[:, :], ALU.mult).then_inc(mask0_s, 1)

            def xl_rest(g):
                if live(g):
                    wait(pool, xl_hi_s, g)
                    wait(pool, av1_s, g - 1, 2)
                    pool.tensor_tensor(xl_lo[:, :], xl[:, 0:HF], xl_hi[:, :], ALU.subtract).then_inc(xl_lo_s, 1)

            def xt_rest(g, c):
                if live(g):
                    wait(pool, xt_hi_s, g)
                    wait(pool, xw1_s, g - 2)
                    pool.tensor_tensor(xt_lo[:, c, :], xt[:, c, :], xt_hi[:, c, :], ALU.subtract).then_inc(xt_lo_s, 1)

            def wh_rest(g):
                if live(g):
                    wait(pool, wh_hi_s, g)
                    wait(pool, av3_s, g - 1)
                    pool.tensor_tensor(wh_lo[:, :], wh[:, :], wh_hi[:, :], ALU.subtract).then_inc(wh_lo_s, 1)

            def x2_rest(g):
                if live(g):
                    wait(pool, x2_hi_s, g)
                    wait(pool, av2_s, g - 1)
                    pool.tensor_tensor(x2_lo[:, :], x2[:, :], x2_hi[:, :], ALU.subtract).then_inc(x2_lo_s, 1)

            def normalise_p1(g):
                if live(g):
                    wait(pool, rden1_s, g)
                    wait(pool, pt1_s, g - 1)
                    pool.tensor_tensor(p1_n[:, :, :], p1[:, :, :], rden1[:, :].unsqueeze(2).broadcast_to([P, H, N]),
                                       ALU.mult).then_inc(p1_n_s, 1)

            def step(i, c):
                wh_rest(i - 3)
                xt_rest(i + 1, 1 - c)
                residual_bias(i - 1, 1 - c)
                xl_rest(i)
                normalise_p1(i)
                residual_relu(i - 3, 1 - c)
                x2_rest(i - 1)
                make_mask0(i + 1, 1 - c)
                if is_step(i, 0):
                    attention_lo(PARTS2)
                    weight_lo(PARTS3)
                if is_step(i, 1):
                    attention_lo(PARTS3)

            xt_rest(0, 0)
            weight_lo(PARTS1)
            attention_lo(PARTS1)
            pool.wait_ge(consts_made, 1)
            make_mask0(0, 0)
            weight_lo(PARTS2)
            pool.wait_ge(bias_in, 2 * 16)
            run(pool, step)


def kernel(x, adj, L0_gnn_W1, L0_gnn_att_src1, L0_gnn_att_dst1, L0_gnn_b1, L0_gnn_W2, L0_gnn_att_src2,
           L0_gnn_att_dst2, L0_gnn_b2, L1_gnn_W, L1_gnn_a):
    import numpy as np
    import concourse.bacc as bacc
    from concourse.bass_utils import run_bass_kernel_spmd

    x, adj = np.asarray(x), np.asarray(adj)
    B, N, D = x.shape
    given = {
        "x": x,
        "x_t": x.reshape(B, N, D // P, P).transpose(0, 3, 2, 1).reshape(B, P, D),
        "adj_t": adj.transpose(0, 2, 1),
        "w1": L0_gnn_W1, "a_src1": L0_gnn_att_src1, "a_dst1": L0_gnn_att_dst1, "b1": L0_gnn_b1,
        "w2": L0_gnn_W2, "a_src2": L0_gnn_att_src2, "a_dst2": L0_gnn_att_dst2, "b2": L0_gnn_b2,
        "w3": L1_gnn_W, "a3": L1_gnn_a,
    }
    nc = bacc.Bacc("TRN2", target_bir_lowering=False, num_devices=1)
    arrays, args = {}, {}
    for name, a in given.items():
        a = np.ascontiguousarray(a)
        arrays[f"in_{name}"] = a
        args[name] = nc.dram_tensor(f"in_{name}", a.shape, mybir.dt.from_np(a.dtype), kind="ExternalInput").ap()
    args["out"] = nc.dram_tensor("out", (B, N, D), F32, kind="ExternalOutput").ap()
    resnorm_gat_kernel(nc, **args)
    r = run_bass_kernel_spmd(nc, [arrays], core_ids=[0])
    return r.results[0]["out"]
```
